# Optimizing a Trainium2 kernel written in Bass

```python
import numpy as np
import jax
import jax.numpy as jnp

def _softmax(x, axis=-1):
    return jax.nn.softmax(x, axis=axis)

def _gelu(x):
    return jax.nn.gelu(x, approximate=True)

def _silu(x):
    return jax.nn.silu(x)

def _sigmoid(x):
    return jax.nn.sigmoid(x)

def _layernorm(x, axis=-1, eps=1e-05):
    m = jnp.mean(x, axis=axis, keepdims=True)
    v = jnp.var(x, axis=axis, keepdims=True)
    return (x - m) / jnp.sqrt(v + eps)

def _scatter_add(tgt, idx, src, axis=0):
    return tgt.at[idx].add(src)

def _segment_sum(src, seg, n):
    return jax.ops.segment_sum(src, seg, n)
kernel_name = 'mk_xattn_seq_d4_seqx_r4_04d732'

def setup_inputs(seed: int=0):
    np.random.seed(seed)
    _w = jnp.asarray

    def _rec_inputs():
        import jax
        import jax.numpy as jnp
        _rk = jax.random.key(seed)
        x = -0.000125 + 0.9999 * jax.random.normal(jax.random.fold_in(_rk, 1), (2, 512, 512), jnp.float32)
        _lenS = 512 - jax.random.randint(jax.random.fold_in(_rk, 7), (2,), 0, max(1, 512 // 4) + 1, jnp.int32)
        _lenS2 = 1024 - jax.random.randint(jax.random.fold_in(_rk, 8), (2,), 0, max(1, 1024 // 4) + 1, jnp.int32)
        _ctx_2048P = jax.random.normal(jax.random.fold_in(_rk, 11), (2, 16, 512), jnp.float32)
        _ctx_2048c = jax.random.dirichlet(jax.random.fold_in(_rk, 511), 0.3 * jnp.ones((16,), jnp.float32), (2, 1024))
        _ctx_2048t = jnp.einsum('bsk,bkd->bsd', _ctx_2048c, _ctx_2048P)
        _ctx_2048t = _ctx_2048t * jax.lax.rsqrt(jnp.mean(jnp.square(_ctx_2048t)) + 1e-12) * 0.953939
        ctx_2048 = -0.00401388 + 1.00018 * (_ctx_2048t + 0.3 * jax.random.normal(jax.random.fold_in(_rk, 611), (2, 1024, 512), jnp.float32))
        _validS = jnp.arange(512)[None, :] < _lenS[:, None]
        _validS2 = jnp.arange(1024)[None, :] < _lenS2[:, None]
        _causal = jnp.tril(jnp.ones((512, 512), dtype=bool))
        mask_Bx1xSxS2_ff0 = jnp.where(jnp.ones((2, 1, 512, 1024), dtype=bool), 0.0, -1000000000.0).astype(jnp.float32)
        mask_BxS2_ik0 = jnp.where(jnp.broadcast_to(_validS2[:, :], (2, 1024)), 0, 1).astype(jnp.int32)
        return (x, ctx_2048, mask_Bx1xSxS2_ff0, mask_BxS2_ik0)
    x, ctx_2048, mask_Bx1xSxS2_ff0, mask_BxS2_ik0 = _rec_inputs()

    def _L0_xattn_setup():
        import jax, jax.numpy as jnp
        import numpy as np
        H = 512
        B, L, S = (4, 1024, 10)
        key = jax.random.key(seed)
        k1, k2, k3, k4, k5, k6 = jax.random.split(key, 6)
        scale = 1.0 / np.sqrt(H)
        return {'h_english': jax.random.normal(k1, (B, L, H), dtype=jnp.float32), 'h_lojban': jax.random.normal(k2, (B, S, H), dtype=jnp.float32), 'w_q': jax.random.normal(k3, (H, H), dtype=jnp.float32) * scale, 'w_k': jax.random.normal(k4, (H, H), dtype=jnp.float32) * scale, 'w_v': jax.random.normal(k5, (H, H), dtype=jnp.float32) * scale, 'w_o': jax.random.normal(k6, (H, H), dtype=jnp.float32) * scale, 'alpha': jnp.float32(0.1)}
    _L0_xattn_all = _L0_xattn_setup()
    _L0_xattn_in = {k: v for k, v in _L0_xattn_all.items() if k in ('w_q', 'w_k', 'w_v', 'w_o', 'alpha')}
    del _L0_xattn_all

    def _L1_xattn_setup():
        import jax, jax.numpy as jnp
        import numpy as np
        H = 512
        NH = 32
        KVH = 8
        HD = H // NH
        GROUPS = NH // KVH
        EPS = 1e-06
        B, L, S = (4, 256, 256)

        def _gqa_forward(hidden_state, encoder_hidden_state, encoder_attention_mask, Wq, bq, Wk, bk, Wv, bv, Wo, bo, gamma, beta):
            b, l, _ = hidden_state.shape
            s = encoder_hidden_state.shape[1]
            q = hidden_state @ Wq + bq
            k = encoder_hidden_state @ Wk + bk
            v = encoder_hidden_state @ Wv + bv
            q = q.reshape(b, l, KVH, GROUPS, HD).transpose(0, 2, 3, 1, 4)
            k = k.reshape(b, s, KVH, HD).transpose(0, 2, 1, 3)
            v = v.reshape(b, s, KVH, HD).transpose(0, 2, 1, 3)
            scale = 1.0 / jnp.sqrt(jnp.asarray(HD, q.dtype))
            scores = jnp.einsum('bkgld,bksd->bkgls', q, k) * scale
            scores = scores + encoder_attention_mask[:, :, None, :, :]
            attn = jax.nn.softmax(scores, axis=-1)
            out = jnp.einsum('bkgls,bksd->bkgld', attn, v)
            out = out.transpose(0, 3, 1, 2, 4).reshape(b, l, H)
            out = out @ Wo + bo
            x = out + hidden_state
            mu = jnp.mean(x, axis=-1, keepdims=True)
            var = jnp.var(x, axis=-1, keepdims=True)
            return (x - mu) * jax.lax.rsqrt(var + EPS) * gamma + beta
        key = jax.random.key(seed)
        ks = jax.random.split(key, 12)
        sd = 0.02
        return {'hidden_state': jax.random.normal(ks[0], (B, L, H), jnp.float32), 'encoder_hidden_state': jax.random.normal(ks[1], (B, S, H), jnp.float32), 'encoder_attention_mask': jnp.zeros((B, 1, L, S), jnp.float32), 'Wq': jax.random.normal(ks[2], (H, H), jnp.float32) * sd, 'bq': jnp.zeros((H,), jnp.float32), 'Wk': jax.random.normal(ks[3], (H, KVH * HD), jnp.float32) * sd, 'bk': jnp.zeros((KVH * HD,), jnp.float32), 'Wv': jax.random.normal(ks[4], (H, KVH * HD), jnp.float32) * sd, 'bv': jnp.zeros((KVH * HD,), jnp.float32), 'Wo': jax.random.normal(ks[5], (H, H), jnp.float32) * sd, 'bo': jnp.zeros((H,), jnp.float32), 'gamma': jnp.ones((H,), jnp.float32), 'beta': jnp.zeros((H,), jnp.float32)}
    _L1_xattn_all = _L1_xattn_setup()
    _L1_xattn_in = {k: v for k, v in _L1_xattn_all.items() if k in ('Wq', 'bq', 'Wk', 'bk', 'Wv', 'bv', 'Wo', 'bo', 'gamma', 'beta')}
    del _L1_xattn_all

    def _L2_xattn_setup():
        import jax, jax.numpy as jnp
        import numpy as np
        B, Q, S1, S2 = (4, 64, 512, 512)
        D, H, K, F = (512, 16, 128, 2048)
        LN_EPS = 1e-05

        def _layer_norm(x, scale, offset):
            mu = jnp.mean(x, axis=-1, keepdims=True)
            var = jnp.var(x, axis=-1, keepdims=True)
            return (x - mu) * jax.lax.rsqrt(var + LN_EPS) * scale + offset

        def _cross_attention(q_in, kv_in, wq, bq, wk, bk, wv, bv, wo, bo, bias_k, bias_v):
            b, q_len, _ = q_in.shape
            t = kv_in.shape[1]
            qh = (q_in @ wq + bq).reshape(b, q_len, H, K)
            kh = (kv_in @ wk + bk).reshape(b, t, H, K)
            vh = (kv_in @ wv + bv).reshape(b, t, H, K)
            kh = jnp.concatenate([kh, jnp.broadcast_to(bias_k, (b, 1, H, K))], axis=1)
            vh = jnp.concatenate([vh, jnp.broadcast_to(bias_v, (b, 1, H, K))], axis=1)
            scale = jnp.sqrt(jnp.asarray(K, q_in.dtype))
            logits = jnp.einsum('bqhk,bthk->bhqt', qh, kh) / scale
            weights = jax.nn.softmax(logits, axis=-1)
            ctx = jnp.einsum('bhqt,bthk->bqhk', weights, vh).reshape(b, q_len, H * K)
            return ctx @ wo + bo

        def _forward(x, xf_1, xf_2, ln1_scale, ln1_offset, wq1, bq1, wk1, bk1, wv1, bv1, wo1, bo1, bias_k1, bias_v1, ln2_scale, ln2_offset, wq2, bq2, wk2, bk2, wv2, bv2, wo2, bo2, bias_k2, bias_v2, ln_mlp_scale, ln_mlp_offset, w_fc1, b_fc1, w_fc2, b_fc2):
            res = x
            h = _layer_norm(x, ln1_scale, ln1_offset)
            x = res + _cross_attention(h, xf_1, wq1, bq1, wk1, bk1, wv1, bv1, wo1, bo1, bias_k1, bias_v1)
            res = x
            h = _layer_norm(x, ln2_scale, ln2_offset)
            x = res + _cross_attention(h, xf_2, wq2, bq2, wk2, bk2, wv2, bv2, wo2, bo2, bias_k2, bias_v2)
            h = _layer_norm(x, ln_mlp_scale, ln_mlp_offset)
            h = jax.nn.gelu(h @ w_fc1 + b_fc1, approximate=False) @ w_fc2 + b_fc2
            return x + h
        key = jax.random.key(seed)
        ks = iter(jax.random.split(key, 64))

        def rn(shape, s=0.02):
            return jax.random.normal(next(ks), shape, jnp.float32) * s
        inp = {'x': rn((B, Q, D), 1.0), 'xf_1': rn((B, S1, D), 1.0), 'xf_2': rn((B, S2, D), 1.0)}
        for i in (1, 2):
            inp[f'ln{i}_scale'] = jnp.ones((D,), jnp.float32)
            inp[f'ln{i}_offset'] = jnp.zeros((D,), jnp.float32)
            inp[f'wq{i}'] = rn((D, H * K))
            inp[f'bq{i}'] = jnp.zeros((H * K,), jnp.float32)
            inp[f'wk{i}'] = rn((D, H * K))
            inp[f'bk{i}'] = jnp.zeros((H * K,), jnp.float32)
            inp[f'wv{i}'] = rn((D, H * K))
            inp[f'bv{i}'] = jnp.zeros((H * K,), jnp.float32)
            inp[f'wo{i}'] = rn((H * K, D))
            inp[f'bo{i}'] = jnp.zeros((D,), jnp.float32)
            inp[f'bias_k{i}'] = rn((1, 1, H, K))
            inp[f'bias_v{i}'] = rn((1, 1, H, K))
        inp['ln_mlp_scale'] = jnp.ones((D,), jnp.float32)
        inp['ln_mlp_offset'] = jnp.zeros((D,), jnp.float32)
        inp['w_fc1'] = rn((D, F))
        inp['b_fc1'] = jnp.zeros((F,), jnp.float32)
        inp['w_fc2'] = rn((F, D))
        inp['b_fc2'] = jnp.zeros((D,), jnp.float32)
        return inp
    _L2_xattn_all = _L2_xattn_setup()
    _L2_xattn_in = {k: v for k, v in _L2_xattn_all.items() if k in ('ln1_scale', 'ln1_offset', 'wq1', 'bq1', 'wk1', 'bk1', 'wv1', 'bv1', 'wo1', 'bo1', 'bias_k1', 'bias_v1', 'ln2_scale', 'ln2_offset', 'wq2', 'bq2', 'wk2', 'bk2', 'wv2', 'bv2', 'wo2', 'bo2', 'bias_k2', 'bias_v2', 'ln_mlp_scale', 'ln_mlp_offset', 'w_fc1', 'b_fc1', 'w_fc2', 'b_fc2')}
    del _L2_xattn_all

    def _L3_xattn_setup():
        import jax, jax.numpy as jnp
        import numpy as np
        B, P, K, H, NH = (4, 512, 64, 512, 16)
        DH = H // NH
        EPS = 1e-06

        def rmsnorm(x, w):
            var = jnp.mean(jnp.square(x), axis=-1, keepdims=True)
            return x * jax.lax.rsqrt(var + EPS) * w
        key = jax.random.key(seed)
        ks = jax.random.split(key, 12)
        s = 0.02
        return {'x': jax.random.normal(ks[0], (B, P, H), jnp.float32), 'latents': jax.random.normal(ks[1], (B, K, H), jnp.float32), 'attention_mask': jax.random.randint(ks[2], (B, P), 0, 2, jnp.int32), 'q_w': s * jax.random.normal(ks[3], (H, H), jnp.float32), 'q_b': jnp.zeros((H,), jnp.float32), 'kv_w': s * jax.random.normal(ks[4], (H, 2 * H), jnp.float32), 'kv_b': jnp.zeros((2 * H,), jnp.float32), 'out_w': s * jax.random.normal(ks[5], (H, H), jnp.float32), 'out_b': jnp.zeros((H,), jnp.float32), 'postnorm_w': jnp.ones((H,), jnp.float32), 'mlp_w1': s * jax.random.normal(ks[6], (H, 4 * H), jnp.float32), 'mlp_b1': jnp.zeros((4 * H,), jnp.float32), 'mlp_w2': s * jax.random.normal(ks[7], (4 * H, H), jnp.float32), 'mlp_b2': jnp.zeros((H,), jnp.float32)}
    _L3_xattn_all = _L3_xattn_setup()
    _L3_xattn_in = {k: v for k, v in _L3_xattn_all.items() if k in ('q_w', 'q_b', 'kv_w', 'kv_b', 'out_w', 'out_b', 'postnorm_w', 'mlp_w1', 'mlp_b1', 'mlp_w2', 'mlp_b2')}
    del _L3_xattn_all
    return {'x': x, 'ctx_2048': ctx_2048, 'mask_Bx1xSxS2_ff0': mask_Bx1xSxS2_ff0, 'mask_BxS2_ik0': mask_BxS2_ik0, 'L0_xattn_w_q': _L0_xattn_in['w_q'], 'L0_xattn_w_k': _L0_xattn_in['w_k'], 'L0_xattn_w_v': _L0_xattn_in['w_v'], 'L0_xattn_w_o': _L0_xattn_in['w_o'], 'L0_xattn_alpha': _L0_xattn_in['alpha'], 'L1_xattn_Wq': _L1_xattn_in['Wq'], 'L1_xattn_bq': _L1_xattn_in['bq'], 'L1_xattn_Wk': _L1_xattn_in['Wk'], 'L1_xattn_bk': _L1_xattn_in['bk'], 'L1_xattn_Wv': _L1_xattn_in['Wv'], 'L1_xattn_bv': _L1_xattn_in['bv'], 'L1_xattn_Wo': _L1_xattn_in['Wo'], 'L1_xattn_bo': _L1_xattn_in['bo'], 'L1_xattn_gamma': _L1_xattn_in['gamma'], 'L1_xattn_beta': _L1_xattn_in['beta'], 'L2_xattn_ln1_scale': _L2_xattn_in['ln1_scale'], 'L2_xattn_ln1_offset': _L2_xattn_in['ln1_offset'], 'L2_xattn_wq1': _L2_xattn_in['wq1'], 'L2_xattn_bq1': _L2_xattn_in['bq1'], 'L2_xattn_wk1': _L2_xattn_in['wk1'], 'L2_xattn_bk1': _L2_xattn_in['bk1'], 'L2_xattn_wv1': _L2_xattn_in['wv1'], 'L2_xattn_bv1': _L2_xattn_in['bv1'], 'L2_xattn_wo1': _L2_xattn_in['wo1'], 'L2_xattn_bo1': _L2_xattn_in['bo1'], 'L2_xattn_bias_k1': _L2_xattn_in['bias_k1'], 'L2_xattn_bias_v1': _L2_xattn_in['bias_v1'], 'L2_xattn_ln2_scale': _L2_xattn_in['ln2_scale'], 'L2_xattn_ln2_offset': _L2_xattn_in['ln2_offset'], 'L2_xattn_wq2': _L2_xattn_in['wq2'], 'L2_xattn_bq2': _L2_xattn_in['bq2'], 'L2_xattn_wk2': _L2_xattn_in['wk2'], 'L2_xattn_bk2': _L2_xattn_in['bk2'], 'L2_xattn_wv2': _L2_xattn_in['wv2'], 'L2_xattn_bv2': _L2_xattn_in['bv2'], 'L2_xattn_wo2': _L2_xattn_in['wo2'], 'L2_xattn_bo2': _L2_xattn_in['bo2'], 'L2_xattn_bias_k2': _L2_xattn_in['bias_k2'], 'L2_xattn_bias_v2': _L2_xattn_in['bias_v2'], 'L2_xattn_ln_mlp_scale': _L2_xattn_in['ln_mlp_scale'], 'L2_xattn_ln_mlp_offset': _L2_xattn_in['ln_mlp_offset'], 'L2_xattn_w_fc1': _L2_xattn_in['w_fc1'], 'L2_xattn_b_fc1': _L2_xattn_in['b_fc1'], 'L2_xattn_w_fc2': _L2_xattn_in['w_fc2'], 'L2_xattn_b_fc2': _L2_xattn_in['b_fc2'], 'L3_xattn_q_w': _L3_xattn_in['q_w'], 'L3_xattn_q_b': _L3_xattn_in['q_b'], 'L3_xattn_kv_w': _L3_xattn_in['kv_w'], 'L3_xattn_kv_b': _L3_xattn_in['kv_b'], 'L3_xattn_out_w': _L3_xattn_in['out_w'], 'L3_xattn_out_b': _L3_xattn_in['out_b'], 'L3_xattn_postnorm_w': _L3_xattn_in['postnorm_w'], 'L3_xattn_mlp_w1': _L3_xattn_in['mlp_w1'], 'L3_xattn_mlp_b1': _L3_xattn_in['mlp_b1'], 'L3_xattn_mlp_w2': _L3_xattn_in['mlp_w2'], 'L3_xattn_mlp_b2': _L3_xattn_in['mlp_b2']}

def reference(x, ctx_2048, mask_Bx1xSxS2_ff0, mask_BxS2_ik0, L0_xattn_w_q, L0_xattn_w_k, L0_xattn_w_v, L0_xattn_w_o, L0_xattn_alpha, L1_xattn_Wq, L1_xattn_bq, L1_xattn_Wk, L1_xattn_bk, L1_xattn_Wv, L1_xattn_bv, L1_xattn_Wo, L1_xattn_bo, L1_xattn_gamma, L1_xattn_beta, L2_xattn_ln1_scale, L2_xattn_ln1_offset, L2_xattn_wq1, L2_xattn_bq1, L2_xattn_wk1, L2_xattn_bk1, L2_xattn_wv1, L2_xattn_bv1, L2_xattn_wo1, L2_xattn_bo1, L2_xattn_bias_k1, L2_xattn_bias_v1, L2_xattn_ln2_scale, L2_xattn_ln2_offset, L2_xattn_wq2, L2_xattn_bq2, L2_xattn_wk2, L2_xattn_bk2, L2_xattn_wv2, L2_xattn_bv2, L2_xattn_wo2, L2_xattn_bo2, L2_xattn_bias_k2, L2_xattn_bias_v2, L2_xattn_ln_mlp_scale, L2_xattn_ln_mlp_offset, L2_xattn_w_fc1, L2_xattn_b_fc1, L2_xattn_w_fc2, L2_xattn_b_fc2, L3_xattn_q_w, L3_xattn_q_b, L3_xattn_kv_w, L3_xattn_kv_b, L3_xattn_out_w, L3_xattn_out_b, L3_xattn_postnorm_w, L3_xattn_mlp_w1, L3_xattn_mlp_b1, L3_xattn_mlp_w2, L3_xattn_mlp_b2):
    import jax
    import jax.numpy as jnp

    def _L0_xattn_ref(h_english, h_lojban, w_q, w_k, w_v, w_o, alpha):
        import jax, jax.numpy as jnp
        import numpy as np
        H = 512
        B, L, S = (4, 1024, 10)
        h = h_english.shape[-1]
        q = jnp.einsum('blh,oh->blo', h_english, w_q)
        k = jnp.einsum('bsh,oh->bso', h_lojban, w_k)
        v = jnp.einsum('bsh,oh->bso', h_lojban, w_v)
        scores = jnp.einsum('blh,bsh->bls', q, k) / jnp.sqrt(jnp.float32(h))
        probs = jax.nn.softmax(scores, axis=-1)
        context = jnp.einsum('bls,bsh->blh', probs, v)
        delta = jnp.einsum('blh,oh->blo', context, w_o)
        return h_english + alpha * delta

    def _L1_xattn_ref(hidden_state, encoder_hidden_state, encoder_attention_mask, Wq, bq, Wk, bk, Wv, bv, Wo, bo, gamma, beta):
        import jax, jax.numpy as jnp
        import numpy as np
        H = 512
        NH = 32
        KVH = 8
        HD = H // NH
        GROUPS = NH // KVH
        EPS = 1e-06
        B, L, S = (4, 256, 256)

        def _gqa_forward(hidden_state, encoder_hidden_state, encoder_attention_mask, Wq, bq, Wk, bk, Wv, bv, Wo, bo, gamma, beta):
            b, l, _ = hidden_state.shape
            s = encoder_hidden_state.shape[1]
            q = hidden_state @ Wq + bq
            k = encoder_hidden_state @ Wk + bk
            v = encoder_hidden_state @ Wv + bv
            q = q.reshape(b, l, KVH, GROUPS, HD).transpose(0, 2, 3, 1, 4)
            k = k.reshape(b, s, KVH, HD).transpose(0, 2, 1, 3)
            v = v.reshape(b, s, KVH, HD).transpose(0, 2, 1, 3)
            scale = 1.0 / jnp.sqrt(jnp.asarray(HD, q.dtype))
            scores = jnp.einsum('bkgld,bksd->bkgls', q, k) * scale
            scores = scores + encoder_attention_mask[:, :, None, :, :]
            attn = jax.nn.softmax(scores, axis=-1)
            out = jnp.einsum('bkgls,bksd->bkgld', attn, v)
            out = out.transpose(0, 3, 1, 2, 4).reshape(b, l, H)
            out = out @ Wo + bo
            x = out + hidden_state
            mu = jnp.mean(x, axis=-1, keepdims=True)
            var = jnp.var(x, axis=-1, keepdims=True)
            return (x - mu) * jax.lax.rsqrt(var + EPS) * gamma + beta
        return _gqa_forward(hidden_state, encoder_hidden_state, encoder_attention_mask, Wq, bq, Wk, bk, Wv, bv, Wo, bo, gamma, beta)

    def _L2_xattn_ref(x, xf_1, xf_2, ln1_scale, ln1_offset, wq1, bq1, wk1, bk1, wv1, bv1, wo1, bo1, bias_k1, bias_v1, ln2_scale, ln2_offset, wq2, bq2, wk2, bk2, wv2, bv2, wo2, bo2, bias_k2, bias_v2, ln_mlp_scale, ln_mlp_offset, w_fc1, b_fc1, w_fc2, b_fc2):
        import jax, jax.numpy as jnp
        import numpy as np
        B, Q, S1, S2 = (4, 64, 512, 512)
        D, H, K, F = (512, 16, 128, 2048)
        LN_EPS = 1e-05

        def _layer_norm(x, scale, offset):
            mu = jnp.mean(x, axis=-1, keepdims=True)
            var = jnp.var(x, axis=-1, keepdims=True)
            return (x - mu) * jax.lax.rsqrt(var + LN_EPS) * scale + offset

        def _cross_attention(q_in, kv_in, wq, bq, wk, bk, wv, bv, wo, bo, bias_k, bias_v):
            b, q_len, _ = q_in.shape
            t = kv_in.shape[1]
            qh = (q_in @ wq + bq).reshape(b, q_len, H, K)
            kh = (kv_in @ wk + bk).reshape(b, t, H, K)
            vh = (kv_in @ wv + bv).reshape(b, t, H, K)
            kh = jnp.concatenate([kh, jnp.broadcast_to(bias_k, (b, 1, H, K))], axis=1)
            vh = jnp.concatenate([vh, jnp.broadcast_to(bias_v, (b, 1, H, K))], axis=1)
            scale = jnp.sqrt(jnp.asarray(K, q_in.dtype))
            logits = jnp.einsum('bqhk,bthk->bhqt', qh, kh) / scale
            weights = jax.nn.softmax(logits, axis=-1)
            ctx = jnp.einsum('bhqt,bthk->bqhk', weights, vh).reshape(b, q_len, H * K)
            return ctx @ wo + bo

        def _forward(x, xf_1, xf_2, ln1_scale, ln1_offset, wq1, bq1, wk1, bk1, wv1, bv1, wo1, bo1, bias_k1, bias_v1, ln2_scale, ln2_offset, wq2, bq2, wk2, bk2, wv2, bv2, wo2, bo2, bias_k2, bias_v2, ln_mlp_scale, ln_mlp_offset, w_fc1, b_fc1, w_fc2, b_fc2):
            res = x
            h = _layer_norm(x, ln1_scale, ln1_offset)
            x = res + _cross_attention(h, xf_1, wq1, bq1, wk1, bk1, wv1, bv1, wo1, bo1, bias_k1, bias_v1)
            res = x
            h = _layer_norm(x, ln2_scale, ln2_offset)
            x = res + _cross_attention(h, xf_2, wq2, bq2, wk2, bk2, wv2, bv2, wo2, bo2, bias_k2, bias_v2)
            h = _layer_norm(x, ln_mlp_scale, ln_mlp_offset)
            h = jax.nn.gelu(h @ w_fc1 + b_fc1, approximate=False) @ w_fc2 + b_fc2
            return x + h
        return _forward(x, xf_1, xf_2, ln1_scale, ln1_offset, wq1, bq1, wk1, bk1, wv1, bv1, wo1, bo1, bias_k1, bias_v1, ln2_scale, ln2_offset, wq2, bq2, wk2, bk2, wv2, bv2, wo2, bo2, bias_k2, bias_v2, ln_mlp_scale, ln_mlp_offset, w_fc1, b_fc1, w_fc2, b_fc2)

    def _L3_xattn_ref(x, latents, attention_mask, q_w, q_b, kv_w, kv_b, out_w, out_b, postnorm_w, mlp_w1, mlp_b1, mlp_w2, mlp_b2):
        import jax, jax.numpy as jnp
        import numpy as np
        B, P, K, H, NH = (4, 512, 64, 512, 16)
        DH = H // NH
        EPS = 1e-06

        def rmsnorm(x, w):
            var = jnp.mean(jnp.square(x), axis=-1, keepdims=True)
            return x * jax.lax.rsqrt(var + EPS) * w
        b, p, _ = x.shape
        k_len = latents.shape[1]
        residual = latents
        h = jnp.concatenate([x, latents], axis=1)
        q = (latents @ q_w + q_b).reshape(b, k_len, NH, DH)
        kv = (h @ kv_w + kv_b).reshape(b, p + k_len, NH, DH, 2)
        kmat, v = (kv[..., 0], kv[..., 1])
        attn = jnp.einsum('bkhd,bnhd->bhkn', q, kmat) / DH
        full_mask = jnp.concatenate([attention_mask.astype(bool), jnp.ones((b, k_len), bool)], axis=-1)
        attn = jnp.where(full_mask[:, None, None, :], attn, -jnp.inf)
        attn = jax.nn.softmax(attn.astype(jnp.float32), axis=-1).astype(q.dtype)
        attn_out = jnp.einsum('bhkn,bnhd->bkhd', attn, v).reshape(b, k_len, H)
        attn_out = attn_out @ out_w + out_b + residual
        out = rmsnorm(attn_out, postnorm_w)
        out = jax.nn.gelu(out @ mlp_w1 + mlp_b1) @ mlp_w2 + mlp_b2
        return out + residual
    x = _L0_xattn_ref(x, ctx_2048, L0_xattn_w_q, L0_xattn_w_k, L0_xattn_w_v, L0_xattn_w_o, L0_xattn_alpha)
    x = _L1_xattn_ref(x, ctx_2048, mask_Bx1xSxS2_ff0, L1_xattn_Wq, L1_xattn_bq, L1_xattn_Wk, L1_xattn_bk, L1_xattn_Wv, L1_xattn_bv, L1_xattn_Wo, L1_xattn_bo, L1_xattn_gamma, L1_xattn_beta)
    x = _L2_xattn_ref(x, ctx_2048, ctx_2048, L2_xattn_ln1_scale, L2_xattn_ln1_offset, L2_xattn_wq1, L2_xattn_bq1, L2_xattn_wk1, L2_xattn_bk1, L2_xattn_wv1, L2_xattn_bv1, L2_xattn_wo1, L2_xattn_bo1, L2_xattn_bias_k1, L2_xattn_bias_v1, L2_xattn_ln2_scale, L2_xattn_ln2_offset, L2_xattn_wq2, L2_xattn_bq2, L2_xattn_wk2, L2_xattn_bk2, L2_xattn_wv2, L2_xattn_bv2, L2_xattn_wo2, L2_xattn_bo2, L2_xattn_bias_k2, L2_xattn_bias_v2, L2_xattn_ln_mlp_scale, L2_xattn_ln_mlp_offset, L2_xattn_w_fc1, L2_xattn_b_fc1, L2_xattn_w_fc2, L2_xattn_b_fc2)
    x = _L3_xattn_ref(ctx_2048, x, mask_BxS2_ik0, L3_xattn_q_w, L3_xattn_q_b, L3_xattn_kv_w, L3_xattn_kv_b, L3_xattn_out_w, L3_xattn_out_b, L3_xattn_postnorm_w, L3_xattn_mlp_w1, L3_xattn_mlp_b1, L3_xattn_mlp_w2, L3_xattn_mlp_b2)
    return x

_drawn_inputs = setup_inputs


def setup_inputs(seed=0):
    import zlib

    import numpy as np

    out = dict(_drawn_inputs(seed))
    spreads = {'L1_xattn_bq': (0.0, 0.8),
     'L1_xattn_bk': (0.0, 2.0),
     'L1_xattn_bv': (0.0, 0.1),
     'L1_xattn_bo': (0.0, 0.1),
     'L1_xattn_gamma': (1.0, 0.2),
     'L1_xattn_beta': (0.0, 0.1),
     'L2_xattn_ln1_scale': (1.0, 0.6),
     'L2_xattn_ln1_offset': (0.0, 0.8),
     'L2_xattn_bq1': (0.0, 0.8),
     'L2_xattn_bk1': (0.0, 2.0),
     'L2_xattn_bv1': (0.0, 0.1),
     'L2_xattn_bo1': (0.0, 0.1),
     'L2_xattn_ln2_scale': (1.0, 0.6),
     'L2_xattn_ln2_offset': (0.0, 0.8),
     'L2_xattn_bq2': (0.0, 0.8),
     'L2_xattn_bk2': (0.0, 2.0),
     'L2_xattn_bv2': (0.0, 0.1),
     'L2_xattn_bo2': (0.0, 0.1),
     'L2_xattn_ln_mlp_scale': (1.0, 0.2),
     'L2_xattn_ln_mlp_offset': (0.0, 0.383),
     'L2_xattn_b_fc1': (0.0, 0.1),
     'L2_xattn_b_fc2': (0.0, 0.1),
     'L3_xattn_q_b': (0.0, 2.0),
     'L3_xattn_kv_b': (0.0, 0.8),
     'L3_xattn_out_b': (0.0, 0.418),
     'L3_xattn_postnorm_w': (1.0, 0.2),
     'L3_xattn_mlp_b1': (0.0, 0.1),
     'L3_xattn_mlp_b2': (0.0, 0.1)}
    factors = {'L0_xattn_w_q': 3.098,
     'L0_xattn_w_k': 3.139,
     'L1_xattn_Wq': 7.87,
     'L1_xattn_Wk': 7.868,
     'L2_xattn_wq1': 3.928,
     'L2_xattn_wk1': 3.793,
     'L2_xattn_bias_k1': 64.0,
     'L2_xattn_bias_v1': 64.0,
     'L2_xattn_wq2': 3.879,
     'L2_xattn_wk2': 3.756,
     'L2_xattn_bias_k2': 64.0,
     'L2_xattn_bias_v2': 64.0,
     'L3_xattn_q_w': 8.0,
     'L3_xattn_kv_w': 4.174,
     'L3_xattn_out_w': 3.639}
    for name, (base, spread) in spreads.items():
        noise = np.random.default_rng([zlib.crc32(name.encode()), seed]).standard_normal(out[name].shape)
        drawn = base * np.exp(spread * noise) if base else spread * noise
        out[name] = jnp.asarray(drawn.astype(out[name].dtype))
    for name, factor in factors.items():
        out[name] = (out[name] * factor).astype(out[name].dtype)
    return out
```

```python
from contextlib import ExitStack

import numpy as np
import concourse.bass as bass
from concourse import mybir

F32 = mybir.dt.float32
F32R = mybir.dt.float32r
I32 = mybir.dt.int32
ACT = mybir.ActivationFunctionType
ALU = mybir.AluOpType
AX = mybir.AxisListType

P = 128
B = 2
NQ = 512
NK = 1024
D = 512
KC = D // P
LT = NQ // P
ST = NK // P
F = 2048
BLOCKED = -3.0e38
ENGINES = 5


TOUCHED = []


def apart(eng):
    eng.sem_inc(TOUCHED[0], 1)


class Slots:

    def __init__(self, sem, name, slots, jobs):
        self.slots, self.jobs = slots, jobs
        self.full = sem(name + "_full")
        self.free = [sem(f"{name}_free{s}") for s in range(slots)]
        self.per = [len(range(s, jobs, slots)) for s in range(slots)]

    def credit(self, eng):
        for f in self.free:
            eng.sem_inc(f, 1)
        eng.sem_inc(self.full, self.jobs)

    def wait_free(self, eng, g, n):
        s = n % self.slots
        eng.wait_ge(self.free[s], g * self.per[s] + (n // self.slots + 1))

    def wait_done(self, eng, g, n):
        s = n % self.slots
        eng.wait_ge(self.free[s], g * self.per[s] + (n // self.slots + 2))

    def wait_full(self, eng, g, n):
        eng.wait_ge(self.full, g * self.jobs + (self.jobs + n + 1))

    def wait_full_before(self, eng, g, n):
        eng.wait_ge(self.full, g * self.jobs + (n + 1))

    def freed(self, n):
        return self.free[n % self.slots]


def build(nc, t, out):
    ctx = ExitStack()
    sems = {}

    def sem(name):
        if name not in sems:
            sems[name] = ctx.enter_context(nc.semaphore(name))
        return sems[name]

    with ctx:
        uid = [0]

        def sb(stack, name, shape, dt=F32):
            uid[0] += 1
            return stack.enter_context(nc.sbuf_tensor(f"{name}_{uid[0]}", shape, dt))

        class Pair:

            def __init__(self, stack, name, shape):
                self.h = sb(stack, name + "_hi", shape, F32R)
                self.l = sb(stack, name + "_lo", shape, F32R)

            def __getitem__(self, key):
                return self.h[key], self.l[key]

        def mm3(pe, o, a, b, start, stop):
            pe.matmul(o, a[0], b[0], start=start, stop=False, skip_group_check=True)
            pe.matmul(o, a[0], b[1], start=False, stop=False, skip_group_check=True)
            return pe.matmul(o, a[1], b[0], start=False, stop=stop, skip_group_check=True)

        def as_f32(ap):
            return ap.bitcast(F32)

        ps = ctx.enter_context(nc.psum_tensor("ps", [P, 8, 512], F32))
        S_BANK, T_BANK, R_BANK = 0, 4, 6

        ident = sb(ctx, "ident", [P, P])
        X = sb(ctx, "X", [P, LT, D])
        XT = Pair(ctx, "XT", [P, KC, NQ])
        CT = Pair(ctx, "CT", [P, KC, NK])
        ones_row = sb(ctx, "ones_row", [1, P], F32R)
        zero_col = sb(ctx, "zero_col", [P, 1])
        alpha = sb(ctx, "alpha", [P, 1])

        vec_rows = []
        at = {}
        n_rows = [0]

        def column(name, src):
            n, w = src.shape
            if n_rows[0] % P + n > P:
                n_rows[0] += P - n_rows[0] % P
            at[name] = n_rows[0]
            vec_rows.append((n_rows[0], n, 0, w, src))
            n_rows[0] += n

        def chunked(name, w=P):
            return t[name].rearrange("(c p) -> c p", p=w)

        column("bq_1", chunked("L1_xattn_bq"))
        column("bk_1", chunked("L1_xattn_bk", 32))
        at["bv_1"] = n_rows[0]
        for grp in range(2):
            for rep in range(4):
                vec_rows.append((n_rows[0], 4, grp * 64 + rep * 16, 16,
                                 t["L1_xattn_bv"].rearrange("(c g d) -> g c d", c=4, g=2)[grp]))
        n_rows[0] += 4
        for i in "12":
            column("lns_" + i, chunked(f"L2_xattn_ln{i}_scale"))
            column("lno_" + i, chunked(f"L2_xattn_ln{i}_offset"))
        column("lns_m", chunked("L2_xattn_ln_mlp_scale"))
        column("lno_m", chunked("L2_xattn_ln_mlp_offset"))
        column("b1_2", chunked("L2_xattn_b_fc1"))
        column("b1_3", chunked("L3_xattn_mlp_b1"))
        column("qb_3", chunked("L3_xattn_q_b"))
        kvb = t["L3_xattn_kv_b"].rearrange("(c p two) -> two c p", p=P, two=2)
        column("kb_3", kvb[0])
        column("vb_3", kvb[1])
        column("pn_3", chunked("L3_xattn_postnorm_w"))
        for i in "12":
            column("bq_2" + i, chunked(f"L2_xattn_bq{i}"))
            column("bk_2" + i, chunked(f"L2_xattn_bk{i}"))
            column("xk_2" + i, t[f"L2_xattn_bias_k{i}"].rearrange("a b h k -> (a b h) k"))
            column("xv_2" + i, t[f"L2_xattn_bias_v{i}"].rearrange("a b h k -> (a b h) k"))
        n_vt = -(-n_rows[0] // P)
        cols = sb(ctx, "cols", [P, n_vt * P])

        s_vec = sem("vectors_loaded")
        s_const = sem("constants_made")
        s_pool = sem("pool_own")
        s_vt = sem("vectors_turned")
        s_cols = sem("columns_ready")
        TOUCHED[:] = [sem("touched")]

        n_stage = [0]
        stage_done = sem("stage_done")

        def new_barrier():
            n_stage[0] += 1
            return n_stage[0]

        def barrier(eng, s, b):
            apart(eng)
            eng.drain().then_inc(stage_done, 1)
            eng.wait_ge(stage_done, b * (n_stage[0] * ENGINES) + s * ENGINES)
            apart(eng)

        credits = []
        extra_credits = []
        stages = []

        def add(sp, pool, pe, act, dve):
            stages.append({"sp": sp, "pool": pool, "pe": pe, "act": act, "dve": dve})

        class Turn:
            turns = {1: 0, 2: 0}

            def __init__(self, src, dst, halves=1, scale=None, shift=None, tmp=None):
                name = f"turn{halves}"
                self.halves, self.nth = halves, Turn.turns[halves]
                Turn.turns[halves] += 1
                self.src, self.dst, self.scale, self.shift, self.tmp = src, dst, scale, shift, tmp
                self.jobs = [(c, h) for h in range(halves) for c in range(KC)]
                self.ring = Slots(sem, name, 2, len(self.jobs))
                self.hi = sem(name + "_hi_done")
                credits.append(self.ring)

            def round_of(self, b):
                return b * Turn.turns[self.halves] + self.nth

            def pe(self, pe, b):
                b = self.round_of(b)
                for n, (c, h) in enumerate(self.jobs):
                    self.ring.wait_free(pe, b, n)
                    for r in range(4):
                        i = pe.transpose(ps[:, T_BANK + n % 2, r * P:(r + 1) * P],
                                         self.src[:, 4 * h + r, c * P:(c + 1) * P], ident[:, :])
                    i.then_inc(self.ring.full, 1)

            def act(self, act, b):
                b = self.round_of(b)
                for n, (c, h) in enumerate(self.jobs):
                    self.ring.wait_full(act, b, n)
                    bank = ps[:, T_BANK + n % 2, :]
                    hi = self.dst.h[:, c, h * 512:(h + 1) * 512]
                    if self.scale is None:
                        act.activation(hi, bank, ACT.Copy).then_inc(self.hi, 1)
                        continue
                    sc = cols[:, self.scale + c:self.scale + c + 1]
                    sh = zero_col[:, :] if self.shift is None else cols[:, self.shift + c:self.shift + c + 1]
                    act.activation(self.tmp[:, n % 2, :], bank, ACT.Identity, bias=sh, scale=sc)
                    act.activation(hi, bank, ACT.Identity, bias=sh, scale=sc).then_inc(self.hi, 1)

            def dve(self, dve, b):
                b = self.round_of(b)
                for n, (c, h) in enumerate(self.jobs):
                    dve.wait_ge(self.hi, b * len(self.jobs) + n + 1)
                    src = ps[:, T_BANK + n % 2, :] if self.scale is None else self.tmp[:, n % 2, :]
                    hi = self.dst.h[:, c, h * 512:(h + 1) * 512]
                    lo = self.dst.l[:, c, h * 512:(h + 1) * 512]
                    dve.tensor_tensor(lo, src, as_f32(hi), ALU.subtract).then_inc(self.ring.freed(n), 1)

        l0 = ExitStack()
        ctx_nat = sb(l0, "ctx_nat", [P, ST, D])
        s_x = sem("x_loaded")
        s_ctx = [sem(f"ctx_loaded{h}") for h in range(2)]
        turn_x = Turn(X, XT)
        turn_c = Turn(ctx_nat, CT, halves=2)
        bar = new_barrier()

        def load_sp(sp, b, s=bar):
            sp.dma_start(X[:, :, :], t["x"][b, :, :].rearrange("(r p) d -> p r d", p=P)).then_inc(s_x, 16)
            c = t["ctx_2048"][b, :, :].rearrange("(h r p) d -> h p r d", p=P, h=2)
            for h in range(2):
                sp.dma_start(ctx_nat[:, 4 * h:4 * h + 4, :], c[h]).then_inc(s_ctx[h], 16)
            barrier(sp, s, b)

        def load_pe(pe, b, s=bar):
            pe.wait_ge(s_x, b * 16 + 16)
            turn_x.pe(pe, b)
            for h in range(2):
                pe.wait_ge(s_ctx[h], b * 16 + 16)
            turn_x.ring.wait_done(pe, turn_x.round_of(b), 2)
            turn_x.ring.wait_done(pe, turn_x.round_of(b), 3)
            turn_c.pe(pe, b)
            barrier(pe, s, b)

        def load_act(act, b, s=bar):
            turn_x.act(act, b)
            turn_c.act(act, b)
            barrier(act, s, b)

        def load_dve(dve, b, s=bar):
            turn_x.dve(dve, b)
            turn_c.dve(dve, b)
            barrier(dve, s, b)

        def load_pool(pool, b, s=bar):
            barrier(pool, s, b)

        add(load_sp, load_pool, load_pe, load_act, load_dve)

        w_nat = sb(l0, "l0_w", [P, 2, KC, D])
        wa = Pair(l0, "l0_wa", [P, KC, D])
        wb = Pair(l0, "l0_wb", [P, KC, D])
        gq = Pair(l0, "l0_g", [P, KC, D])
        yt = Pair(l0, "l0_y", [P, KC, NQ])
        cn = Pair(l0, "l0_cn", [P, 2, D])
        l0_p = sb(l0, "l0_p", [P, LT, NK])
        l0_pt = Pair(l0, "l0_pt", [P, 2, NQ])
        l0_mx = sb(l0, "l0_mx", [P, LT])
        l0_nm = sb(l0, "l0_nm", [P, LT])
        l0_z = sb(l0, "l0_z", [P, LT])
        l0_r = sb(l0, "l0_r", [P, LT])
        l0_ra = sb(l0, "l0_ra", [P, LT])
        SC0 = float(1.0 / np.sqrt(np.float32(D)))
        w0 = [sem(f"l0_w_loaded{i}") for i in range(4)]
        w0s = sem("l0_w_split")
        w0h = sem("l0_w_hi")
        r0 = Slots(sem, "l0_ring", 2, 16)
        r0h = sem("l0_ring_hi")
        wt0 = Slots(sem, "l0_turn_wo", 2, 4)
        wt0h = sem("l0_turn_wo_hi")
        t0 = Slots(sem, "l0_turn_p", 2, ST)
        t0h = sem("l0_turn_p_hi")
        pv0 = sem("l0_pv_tile")
        s0 = Slots(sem, "l0_s", 2, LT)
        m0 = sem("l0_max")
        d0 = sem("l0_dve_own")
        cn0 = sem("l0_cn_split")
        cn0h = sem("l0_cn_hi")
        c0 = sem("l0_ctx_full")
        c0h = sem("l0_ctx_hi")
        c0l = sem("l0_ctx_split")
        credits += [r0, wt0, t0, s0]
        bar = new_barrier()
        W0 = ["L0_xattn_w_q", "L0_xattn_w_k", "L0_xattn_w_v", "L0_xattn_w_o"]

        def l0_sp(sp, b, s=bar):
            for i, name in enumerate(W0):
                if i == 2:
                    sp.wait_ge(w0s, b * 3 + 1)
                if i == 3:
                    sp.wait_ge(w0s, b * 3 + 2)
                sp.dma_start(w_nat[:, i % 2, :, :], t[name].rearrange("(c p) n -> p c n", p=P)).then_inc(w0[i], 16)
            barrier(sp, s, b)

        def l0_pool(pool, b, s=bar):
            for i, dst in enumerate((wa, wb, wa)):
                pool.wait_ge(w0[i], b * 16 + 16)
                if i == 2:
                    r0.wait_full(pool, b, 3)
                apart(pool)
                pool.tensor_copy(dst.h[:, :, :], w_nat[:, i % 2, :, :]).then_inc(w0h, 1)
                pool.wait_ge(w0h, b * 3 + i + 1)
                pool.tensor_tensor(dst.l[:, :, :], w_nat[:, i % 2, :, :], as_f32(dst.h[:, :, :]),
                                   ALU.subtract).then_inc(w0s, 1)
            barrier(pool, s, b)

        def l0_pe(pe, b, s=bar):
            pe.wait_ge(w0s, b * 3 + 2)
            def chunk_jobs(n0, dst_cols, a, bb):
                for m in range(4):
                    n = n0 + m
                    r0.wait_free(pe, b, n)
                    for k in range(KC):
                        i = mm3(pe, ps[:, R_BANK + n % 2, :], a[:, k, m * P:(m + 1) * P], bb[:, k, :],
                                k == 0, k == KC - 1)
                    i.then_inc(r0.full, 1)
                return i
            chunk_jobs(0, None, wa, wb)
            r0.wait_done(pe, b, 2)
            r0.wait_done(pe, b, 3)
            pe.wait_ge(w0[3], b * 16 + 16)
            for n in range(4):
                wt0.wait_free(pe, b, n)
                for r in range(4):
                    i = pe.transpose(ps[:, T_BANK + n % 2, r * P:(r + 1) * P],
                                     w_nat[:, 1, r, n * P:(n + 1) * P], ident[:, :])
                i.then_inc(wt0.full, 1)
            chunk_jobs(4, None, gq, XT)
            r0.wait_done(pe, b, 6)
            r0.wait_done(pe, b, 7)
            for lt in range(LT):
                s0.wait_free(pe, b, lt)
                for hf in range(2):
                    for k in range(KC):
                        i = mm3(pe, ps[:, S_BANK + 2 * (lt % 2) + hf, :], yt[:, k, lt * P:(lt + 1) * P],
                                CT[:, k, hf * 512:(hf + 1) * 512], k == 0, k == KC - 1)
                i.then_inc(s0.full, 1)
            pe.wait_ge(w0s, b * 3 + 3)
            wt0.wait_done(pe, b, 2)
            wt0.wait_done(pe, b, 3)
            chunk_jobs(8, None, wa, wb)
            s0.wait_done(pe, b, LT - 2)
            s0.wait_done(pe, b, LT - 1)
            for st in range(ST + 1):
                if st < ST:
                    t0.wait_free(pe, b, st)
                    for lt in range(LT):
                        i = pe.transpose(ps[:, T_BANK + st % 2, lt * P:(lt + 1) * P],
                                         l0_p[:, lt, st * P:(st + 1) * P], ident[:, :])
                    i.then_inc(t0.full, 1)
                if st:
                    v = st - 1
                    t0.wait_done(pe, b, v)
                    pe.wait_ge(cn0, b * ST + v + 1)
                    for m in range(4):
                        i = mm3(pe, ps[:, S_BANK + m, :], cn[:, v % 2, m * P:(m + 1) * P],
                                l0_pt[:, v % 2, :], v == 0, v == ST - 1)
                    i.then_inc(pv0, 1)
            pe.wait_ge(c0l, b * 4 + 4)
            r0.wait_done(pe, b, 10)
            r0.wait_done(pe, b, 11)
            for lt in range(LT):
                n = 12 + lt
                r0.wait_free(pe, b, n)
                for k in range(KC):
                    i = mm3(pe, ps[:, R_BANK + n % 2, :], yt[:, k, lt * P:(lt + 1) * P], gq[:, k, :],
                            k == 0, k == KC - 1)
                i.then_inc(r0.full, 1)
            barrier(pe, s, b)

        def l0_act(act, b, s=bar):
            def split(n, dst, m):
                r0.wait_full(act, b, n)
                act.activation(dst.h[:, m, :], ps[:, R_BANK + n % 2, :], ACT.Copy).then_inc(r0h, 1)
            for m in range(4):
                split(m, gq, m)
            for n in range(4):
                wt0.wait_full(act, b, n)
                act.activation(wb.h[:, n, :], ps[:, T_BANK + n % 2, :], ACT.Copy).then_inc(wt0h, 1)
            for m in range(4):
                split(4 + m, yt, m)
            for lt in range(LT):
                act.wait_ge(m0, b * LT + lt + 1)
                act.activation(l0_p[:, lt, :], ps[:, S_BANK + 2 * (lt % 2):S_BANK + 2 * (lt % 2) + 2, :], ACT.Exp,
                               bias=l0_nm[:, lt:lt + 1], scale=SC0,
                               accum_out=l0_z[:, lt:lt + 1]).then_inc(s0.freed(lt), 1)
            for m in range(4):
                split(8 + m, gq, m)
            for st in range(ST):
                if st >= 2:
                    act.wait_ge(pv0, b * ST + st - 1)
                act.activation(cn.h[:, st % 2, :], ctx_nat[:, st, :], ACT.Copy).then_inc(cn0h, 1)
                t0.wait_full(act, b, st)
                act.activation(l0_pt.h[:, st % 2, :], ps[:, T_BANK + st % 2, :], ACT.Copy).then_inc(t0h, 1)
            act.wait_ge(pv0, b * ST + ST)
            for m in range(4):
                act.activation(yt.h[:, m, :], ps[:, S_BANK + m, :], ACT.Copy).then_inc(c0h, 1)
            barrier(act, s, b)

        def l0_dve(dve, b, s=bar):
            def lo(n, dst, m):
                dve.wait_ge(r0h, b * 12 + n + 1)
                dve.tensor_tensor(dst.l[:, m, :], ps[:, R_BANK + n % 2, :], as_f32(dst.h[:, m, :]),
                                  ALU.subtract).then_inc(r0.freed(n), 1)
            for m in range(4):
                lo(m, gq, m)
            for n in range(4):
                dve.wait_ge(wt0h, b * 4 + n + 1)
                dve.tensor_tensor(wb.l[:, n, :], ps[:, T_BANK + n % 2, :], as_f32(wb.h[:, n, :]),
                                  ALU.subtract).then_inc(wt0.freed(n), 1)
            for m in range(4):
                lo(4 + m, yt, m)
            for lt in range(LT):
                s0.wait_full(dve, b, lt)
                dve.tensor_reduce(l0_mx[:, lt:lt + 1], ps[:, S_BANK + 2 * (lt % 2):S_BANK + 2 * (lt % 2) + 2, :],
                                  AX.XY, ALU.max).then_inc(d0, 1)
                dve.wait_ge(d0, b * LT + lt + 1)
                dve.tensor_scalar(l0_nm[:, lt:lt + 1], l0_mx[:, lt:lt + 1], -SC0, None, ALU.mult).then_inc(m0, 1)
            for m in range(4):
                lo(8 + m, gq, m)
            for st in range(ST):
                dve.wait_ge(cn0h, b * ST + st + 1)
                dve.tensor_tensor(cn.l[:, st % 2, :], ctx_nat[:, st, :], as_f32(cn.h[:, st % 2, :]),
                                  ALU.subtract).then_inc(cn0, 1)
                dve.wait_ge(t0h, b * ST + st + 1)
                dve.tensor_tensor(l0_pt.l[:, st % 2, :], ps[:, T_BANK + st % 2, :], as_f32(l0_pt.h[:, st % 2, :]),
                                  ALU.subtract).then_inc(t0.freed(st), 1)
            for m in range(4):
                dve.wait_ge(c0h, b * 4 + m + 1)
                dve.tensor_tensor(yt.l[:, m, :], ps[:, S_BANK + m, :], as_f32(yt.h[:, m, :]),
                                  ALU.subtract).then_inc(c0l, 1)
            dve.reciprocal(l0_r[:, :], l0_z[:, :])
            dve.drain()
            dve.tensor_scalar(l0_ra[:, :], l0_r[:, :], alpha[:, 0:1], None, ALU.mult)
            dve.drain()
            for lt in range(LT):
                n = 12 + lt
                r0.wait_full(dve, b, n)
                dve.scalar_tensor_tensor(out=X[:, lt, :], in0=ps[:, R_BANK + n % 2, :], scalar=l0_ra[:, lt:lt + 1],
                                         in1=X[:, lt, :], op0=ALU.mult, op1=ALU.add).then_inc(r0.freed(n), 1)
            barrier(dve, s, b)

        add(l0_sp, l0_pool, l0_pe, l0_act, l0_dve)
        l0.close()

        def narrow(tag, acc, dh, rep, keys, scale, c_bq, c_bk, c_bv, w_q, w_k, w_v, w_o, bo, row_mask):
            own = ExitStack()
            C = D // P
            heads = P // dh
            kw = P // rep
            R = 4 * dh
            two = R == 64
            n_st, n_hf = keys // P, keys // 512
            s_slots = 2 if n_hf == 2 else 1
            n_qs = heads // 2 if two else heads
            n_ks = 1 if two else heads
            order = [u // 2 + (u % 2) * n_qs for u in range(heads)] if two else list(range(heads))

            wk, wv = (Pair(own, tag + n, [P, KC, kw]) for n in ("_wk", "_wv"))
            wq, wo = Pair(own, tag + "_wq", [P, KC, P]), Pair(own, tag + "_wo", [P, D])
            raw_q, raw_o = sb(own, tag + "_raw_q", [P, KC, P]), sb(own, tag + "_raw_o", [P, D])
            raw_kv = sb(own, tag + "_raw_kv", [P, KC, 2 * kw])
            qd, kd = Pair(own, tag + "_q", [P, NQ]), Pair(own, tag + "_k", [kw, keys])
            vd = sb(own, tag + "_v", [P, n_st, kw])
            qs = sb(own, tag + "_qs", [P, 2, NQ], F32R)
            ks = sb(own, tag + "_ks", [P, 1 if two else 2, keys], F32R)
            sel_q, sel_k = Pair(own, tag + "_selq", [P, n_qs, P]), Pair(own, tag + "_selk", [kw, n_ks, P])
            prob = sb(own, tag + "_p", [P, 2, LT, keys])
            pt = sb(own, tag + "_pt", [P, 4, NQ])
            attn = sb(own, tag + "_attn", [P, LT, P])
            att = Pair(own, tag + "_att", [P, NQ])
            madd = sb(own, tag + "_mask", [P, LT if row_mask else 1, keys])
            mint = prob[:, 1, 0, 0:NK].bitcast(I32)
            brow = prob[:, 1, 1, 0:D]
            mx, nm, z, rz = (sb(own, tag + n, [P, 2, LT]) for n in ("_mx", "_nm", "_z", "_rz"))

            plan, n = [], 0
            def ring_step(*x):
                nonlocal n
                plan.append(x + (n,))
                n += 1
                return n - 1
            k_job = [ring_step("k", h) for h in range(n_hf)]
            q_job = ring_step("q")
            v_job = [ring_step("v", v) for v in range(n_st // 4)]
            ks_job, qs_job, out_job, nt = {}, {}, {}, 0
            if two:
                for h in range(n_hf):
                    ks_job[0, h] = ring_step("ks", 0, h)
            for u in range(heads + 1):
                if u < heads and not two:
                    for h in range(n_hf):
                        ks_job[u, h] = ring_step("ks", u, h)
                if u < heads and (not two or u % 2 == 0):
                    qs_job[u // 2 if two else u] = ring_step("qs", u // 2 if two else u)
                if u:
                    out_job[u - 1] = n
                    n += 1
                for lt in range(LT):
                    if u < heads:
                        plan.append(("s", u, lt))
                    if u:
                        for v in range(lt * n_st // LT, (lt + 1) * n_st // LT):
                            plan.append(("t", u - 1, v, nt))
                            if v >= 2:
                                plan.append(("pv", u - 1, v - 2, nt - 2))
                            nt += 1
                if u:
                    plan.append(("pv", u - 1, n_st - 2, nt - 2))
                    plan.append(("pv", u - 1, n_st - 1, nt - 1))
            o_job = list(range(n, n + LT))
            n += LT

            ring = Slots(sem, tag + "_ring", 2, n)
            ring_hi = sem(tag + "_ring_hi")
            turn = Slots(sem, tag + "_turn", 2, nt + 1)
            turn_hi = sem(tag + "_turn_hi")
            score = Slots(sem, tag + "_score", s_slots, heads * LT)
            max_done, exp_done = sem(tag + "_max_done"), sem(tag + "_exp_done")
            recip_done = sem(tag + "_recip_done")
            NS = heads * LT
            loaded = {k: sem(f"{tag}_loaded_{k}") for k in ("kqobm" if w_v is None else "kvqobm")}
            split = {k: sem(f"{tag}_split_{k}") for k in "kqvo"}
            pool_hi = sem(tag + "_pool_hi")
            sel_done = sem(tag + "_selections_made")
            last_use = {"k": k_job[-1], "q": q_job, "v": v_job[-1], "o": o_job[-1]}
            credits.extend([ring, turn, score])
            extra_credits.extend(split.values())
            done = new_barrier()
            bank = lambda m: ps[:, R_BANK + m % 2, :]

            def sp_(sp, b):
                sp.dma_start(brow, bo.unsqueeze(0).broadcast_to([P, D])).then_inc(loaded["b"], 16)
                if row_mask:
                    sp.dma_start(madd[:, :, :], t["mask_Bx1xSxS2_ff0"][b, 0, :, :].rearrange("(r p) s -> p r s", p=P)
                                 ).then_inc(loaded["m"], 16)
                else:
                    sp.dma_start(mint, t["mask_BxS2_ik0"][b, :].unsqueeze(0).broadcast_to([P, NK])
                                 ).then_inc(loaded["m"], 16)
                with sp.Fori(0, C) as c:
                    g = b * C + c
                    sp.wait_ge(split["k"], g + 1)
                    sp.wait_ge(split["v"], g + 1)
                    if w_v is None:
                        sp.dma_start(raw_kv[:, :, :], w_k.rearrange("(k p) (c n) -> c p k n", p=P, n=2 * kw)[c, :, :, :]
                                     ).then_inc(loaded["k"], 16)
                    else:
                        sp.dma_start(raw_kv[:, :, 0:kw], w_k.rearrange("(k p) (c n) -> c p k n", p=P, n=kw)[c, :, :, :]
                                     ).then_inc(loaded["k"], 16)
                        sp.dma_start(raw_kv[:, :, kw:2 * kw], w_v.rearrange("(k p) (c n) -> c p k n", p=P, n=kw)[c, :, :, :]
                                     ).then_inc(loaded["v"], 16)
                    sp.wait_ge(split["q"], g + 1)
                    sp.dma_start(raw_q[:, :, :], w_q.rearrange("(k p) (c n) -> c p k n", p=P, n=P)[c, :, :, :]
                                 ).then_inc(loaded["q"], 16)
                    sp.wait_ge(split["o"], g + 1)
                    sp.dma_start(raw_o[:, :], w_o.rearrange("(c p) n -> c p n", p=P)[c, :, :]).then_inc(loaded["o"], 16)
                barrier(sp, done, b)

            def pool_(pool, b):
                for m in (sel_q, sel_k):
                    pool.memset(as_f32(m.h[:, :, :]), 0.0)
                    pool.memset(as_f32(m.l[:, :, :]), 0.0)
                pool.drain()
                for blk in range(4):
                    for half in range(2 if two else 1):
                        at_ = half * R + blk * dh
                        for i in range(n_qs):
                            dst, j = (sel_q.h if blk in (0, 2) else sel_q.l), i + half * n_qs
                            pool.tensor_scalar(dst[:, i, at_:at_ + dh], ident[:, j * dh:(j + 1) * dh], float(scale),
                                               None, ALU.mult)
                        for i in range(n_ks):
                            dst, j = (sel_k.h if blk in (0, 1) else sel_k.l), i + half
                            pool.tensor_copy(dst[:, i, at_:at_ + dh], ident[0:kw, j * dh:(j + 1) * dh])
                pool.drain().then_inc(sel_done, 1)
                with pool.Fori(0, C) as c:
                    g = b * C + c
                    if w_v is None:
                        mixed = raw_kv[:, :, :].rearrange("p k (n two) -> p k n two", two=2)
                        src_k, src_v = mixed[:, :, :, 0], mixed[:, :, :, 1]
                    else:
                        src_k, src_v = raw_kv[:, :, 0:kw], raw_kv[:, :, kw:2 * kw]
                    jobs = [("k", "k", wk[:, :, :], src_k), ("q", "q", wq[:, :, :], raw_q[:, :, :]),
                            ("v", "k" if w_v is None else "v", wv[:, :, :], src_v), ("o", "o", wo[:, :], raw_o[:, :])]
                    for i, (name, load, (hi, lo), src) in enumerate(jobs):
                        pool.wait_ge(loaded[load], g * 16 + 16)
                        ring.wait_full_before(pool, g, last_use[name])
                        apart(pool)
                        pool.tensor_copy(hi, src).then_inc(pool_hi, 1)
                        pool.wait_ge(pool_hi, g * 4 + i + 1)
                        pool.tensor_tensor(lo, src, as_f32(hi), ALU.subtract).then_inc(split[name], 1)
                barrier(pool, done, b)

            def keys_of(k, h):
                return CT[:, k, h * 512:(h + 1) * 512] if h < 2 else XT[:, k, :]

            def key_tile(k, st):
                return CT[:, k, st * P:(st + 1) * P] if st < ST else XT[:, k, (st - ST) * P:(st - ST + 1) * P]

            def pe_(pe, b):
                pe.wait_ge(sel_done, b + 1)
                apart(pe)
                with pe.Fori(0, C) as c:
                    g = b * C + c
                    for x in plan:
                        if x[0] == "k":
                            if x[1] == 0:
                                pe.wait_ge(split["k"], g + 2)
                            ring.wait_free(pe, g, x[-1])
                            for k in range(KC):
                                i = mm3(pe, bank(x[-1])[0:kw, :], wk[:, k, :], keys_of(k, x[1]), k == 0, k == KC - 1)
                            i.then_inc(ring.full, 1)
                        elif x[0] == "q":
                            pe.wait_ge(split["q"], g + 2)
                            ring.wait_free(pe, g, x[-1])
                            for k in range(KC):
                                i = mm3(pe, bank(x[-1]), wq[:, k, :], XT[:, k, :], k == 0, k == KC - 1)
                            i.then_inc(ring.full, 1)
                        elif x[0] == "v":
                            if x[1] == 0:
                                pe.wait_ge(split["v"], g + 2)
                            ring.wait_free(pe, g, x[-1])
                            for q in range(4):
                                for k in range(KC):
                                    i = mm3(pe, bank(x[-1])[:, q * kw:(q + 1) * kw], key_tile(k, 4 * x[1] + q),
                                            wv[:, k, :], k == 0 and q == 0, k == KC - 1)
                            i.then_inc(ring.full, 1)
                        elif x[0] == "ks":
                            _, u, h, m = x
                            if u == 0:
                                ring.wait_done(pe, g, k_job[h])
                            ring.wait_free(pe, g, m)
                            pe.matmul(bank(m), sel_k.h[:, u, :], kd.h[:, h * 512:(h + 1) * 512], start=True,
                                      stop=False, skip_group_check=True)
                            pe.matmul(bank(m), sel_k.l[:, u, :], kd.l[:, h * 512:(h + 1) * 512], start=False,
                                      stop=True, skip_group_check=True).then_inc(ring.full, 1)
                        elif x[0] == "qs":
                            _, u, m = x
                            if u == 0:
                                ring.wait_done(pe, g, q_job)
                            ring.wait_free(pe, g, m)
                            pe.matmul(bank(m), sel_q.h[:, u, :], qd.h[:, :], start=True, stop=False,
                                      skip_group_check=True)
                            pe.matmul(bank(m), sel_q.l[:, u, :], qd.l[:, :], start=False, stop=True,
                                      skip_group_check=True).then_inc(ring.full, 1)
                        elif x[0] == "s":
                            _, u, lt = x
                            if lt == 0:
                                ring.wait_done(pe, g, qs_job[u // 2 if two else u])
                                for h in range(n_hf):
                                    ring.wait_done(pe, g, ks_job[0 if two else u, h])
                            m = u * LT + lt
                            score.wait_free(pe, g, m)
                            p0 = 64 * (u % 2) if two else 0
                            for h in range(n_hf):
                                i = pe.matmul(ps[:, S_BANK + 2 * (m % s_slots) + h, :],
                                              qs[p0:p0 + R, (u // 2 if two else u) % 2, lt * P:(lt + 1) * P],
                                              ks[p0:p0 + R, 0 if two else u % 2, h * 512:(h + 1) * 512],
                                              start=True, stop=True, skip_group_check=True)
                            i.then_inc(score.full, 1)
                        elif x[0] == "t":
                            _, u, v, m = x
                            if v == 0:
                                pe.wait_ge(exp_done, g * NS + u * LT + LT)
                            turn.wait_free(pe, g, m)
                            for lt in range(LT):
                                i = pe.transpose(ps[:, T_BANK + m % 2, lt * P:(lt + 1) * P],
                                                 prob[:, u % 2, lt, v * P:(v + 1) * P], ident[:, :])
                            i.then_inc(turn.full, 1)
                        else:
                            _, u, v, m = x
                            if v == 0:
                                ring.wait_free(pe, g, out_job[u])
                                if u == 0:
                                    for j in v_job:
                                        ring.wait_done(pe, g, j)
                            turn.wait_done(pe, g, m)
                            kv = order[u] // rep * dh
                            for lt in range(LT):
                                i = pe.matmul(bank(out_job[u])[:, lt * dh:(lt + 1) * dh],
                                              pt[:, m % 4, lt * P:(lt + 1) * P], vd[:, v, kv:kv + dh],
                                              start=(v == 0 and lt == 0), stop=(v == n_st - 1),
                                              skip_group_check=True)
                            if v == n_st - 1:
                                i.then_inc(ring.full, 1)
                    ring.wait_done(pe, g, out_job[heads - 1])
                    ring.wait_done(pe, g, out_job[heads - 2])
                    turn.wait_free(pe, g, nt)
                    for lt in range(LT):
                        i = pe.transpose(ps[:, T_BANK + nt % 2, lt * P:(lt + 1) * P], attn[:, lt, :], ident[:, :])
                    i.then_inc(turn.full, 1)
                    pe.wait_ge(split["o"], g + 2)
                    turn.wait_done(pe, g, nt)
                    for lt in range(LT):
                        ring.wait_free(pe, g, o_job[lt])
                        mm3(pe, bank(o_job[lt]), att[:, lt * P:(lt + 1) * P], wo[:, :], True,
                            True).then_inc(ring.full, 1)
                barrier(pe, done, b)

            def by_act(m):
                return m % 2 == 0

            def act_(act, b):
                with act.Fori(0, C) as c:
                    g = b * C + c
                    for x in plan:
                        if x[0] == "k":
                            ring.wait_full(act, g, x[-1])
                            apart(act)
                            act.activation(kd.h[:, x[1] * 512:(x[1] + 1) * 512], bank(x[-1])[0:kw, :], ACT.Identity,
                                           bias=cols[0:kw, bass.ds(c + c_bk, 1)]).then_inc(ring_hi, 1)
                        elif x[0] == "q":
                            ring.wait_full(act, g, x[-1])
                            apart(act)
                            act.activation(qd.h[:, :], bank(x[-1]), ACT.Identity,
                                           bias=cols[:, bass.ds(c + c_bq, 1)]).then_inc(ring_hi, 1)
                        elif x[0] == "ks":
                            _, u, h, m = x
                            ring.wait_full(act, g, m)
                            act.activation(ks[:, u % 2, h * 512:(h + 1) * 512], bank(m),
                                           ACT.Copy).then_inc(ring.freed(m), 1)
                        elif x[0] == "qs":
                            ring.wait_full(act, g, x[-1])
                            act.activation(qs[:, x[1] % 2, :], bank(x[-1]), ACT.Copy).then_inc(ring.freed(x[-1]), 1)
                        elif x[0] == "s":
                            _, u, lt = x
                            act.wait_ge(max_done, g * NS + u * LT + lt + 1)
                            act.activation(prob[:, u % 2, lt, :], prob[:, u % 2, lt, :], ACT.Exp,
                                           bias=nm[:, u % 2, lt:lt + 1], scale=1.0,
                                           accum_out=z[:, u % 2, lt:lt + 1]).then_inc(exp_done, 1)
                        elif x[0] == "t" and by_act(x[-1]):
                            m = x[-1]
                            turn.wait_full(act, g, m)
                            act.activation(pt[:, m % 4, :], ps[:, T_BANK + m % 2, :],
                                           ACT.Copy).then_inc(turn.freed(m), 1)
                    turn.wait_full(act, g, nt)
                    apart(act)
                    act.activation(att.h[:, :], ps[:, T_BANK + nt % 2, :], ACT.Identity,
                                   bias=cols[:, bass.ds(c + c_bv, 1)]).then_inc(turn_hi, 1)
                barrier(act, done, b)

            def dve_(dve, b):
                dve.wait_ge(loaded["b"], b * 16 + 16)
                for lt in range(LT):
                    dve.tensor_tensor(acc[:, lt, :], X[:, lt, :], brow, ALU.add)
                dve.wait_ge(loaded["m"], b * 16 + 16)
                apart(dve)
                if not row_mask:
                    dve.tensor_scalar(madd[:, 0, 0:NK], mint, 0.0, BLOCKED, ALU.is_equal, ALU.mult)
                    dve.memset(madd[:, 0, NK:keys], 0.0)
                dve.drain()
                with dve.Fori(0, C) as c:
                    g = b * C + c
                    n_hi = 0
                    for x in plan:
                        if x[0] == "k":
                            n_hi += 1
                            dve.wait_ge(ring_hi, g * (n_hf + 1) + n_hi)
                            sl = slice(x[1] * 512, (x[1] + 1) * 512)
                            dve.scalar_tensor_tensor(out=kd.l[:, sl], in0=bank(x[-1])[0:kw, :],
                                                     scalar=cols[0:kw, bass.ds(c + c_bk, 1)],
                                                     in1=as_f32(kd.h[:, sl]), op0=ALU.add,
                                                     op1=ALU.subtract).then_inc(ring.freed(x[-1]), 1)
                        elif x[0] == "q":
                            n_hi += 1
                            dve.wait_ge(ring_hi, g * (n_hf + 1) + n_hi)
                            dve.scalar_tensor_tensor(out=qd.l[:, :], in0=bank(x[-1]),
                                                     scalar=cols[:, bass.ds(c + c_bq, 1)],
                                                     in1=as_f32(qd.h[:, :]), op0=ALU.add,
                                                     op1=ALU.subtract).then_inc(ring.freed(x[-1]), 1)
                        elif x[0] == "v":
                            ring.wait_full(dve, g, x[-1])
                            dve.tensor_copy(vd[:, 4 * x[1]:4 * x[1] + 4, :],
                                            bank(x[-1])[:, 0:4 * kw].rearrange("p (q w) -> p q w", q=4)
                                            ).then_inc(ring.freed(x[-1]), 1)
                        elif x[0] == "s":
                            _, u, lt = x
                            m = u * LT + lt
                            score.wait_full(dve, g, m)
                            s0_ = S_BANK + 2 * (m % s_slots)
                            apart(dve)
                            dve.tensor_tensor_reduce(
                                prob[:, u % 2, lt, :].rearrange("p (h w) -> p h w", h=n_hf), ps[:, s0_:s0_ + n_hf, :],
                                madd[:, lt if row_mask else 0, :].rearrange("p (h w) -> p h w", h=n_hf),
                                1.0, BLOCKED, ALU.add, ALU.max, mx[:, u % 2, lt:lt + 1]).then_inc(score.freed(m), 1)
                            score.wait_done(dve, g, m)
                            dve.tensor_scalar(nm[:, u % 2, lt:lt + 1], mx[:, u % 2, lt:lt + 1], -1.0, None,
                                              ALU.mult).then_inc(max_done, 1)
                        elif x[0] == "t" and not by_act(x[-1]):
                            m = x[-1]
                            turn.wait_full(dve, g, m)
                            dve.tensor_copy(pt[:, m % 4, :], ps[:, T_BANK + m % 2, :]).then_inc(turn.freed(m), 1)
                        elif x[0] == "pv" and x[2] == n_st - 1:
                            _, u, v, m = x
                            dve.wait_ge(exp_done, g * NS + u * LT + LT)
                            dve.reciprocal(rz[:, u % 2, :], z[:, u % 2, :]).then_inc(recip_done, 1)
                            dve.wait_ge(recip_done, g * heads + u + 1)
                            ring.wait_full(dve, g, out_job[u])
                            dve.tensor_tensor(attn[:, :, order[u] * dh:(order[u] + 1) * dh],
                                              bank(out_job[u])[:, 0:LT * dh].rearrange("p (l d) -> p l d", l=LT),
                                              rz[:, u % 2, :].unsqueeze(2).broadcast_to([P, LT, dh]),
                                              ALU.mult).then_inc(ring.freed(out_job[u]), 1)
                    dve.wait_ge(turn_hi, g + 1)
                    dve.scalar_tensor_tensor(out=att.l[:, :], in0=ps[:, T_BANK + nt % 2, :],
                                             scalar=cols[:, bass.ds(c + c_bv, 1)], in1=as_f32(att.h[:, :]),
                                             op0=ALU.add, op1=ALU.subtract).then_inc(turn.freed(nt), 1)
                    for lt in range(LT):
                        ring.wait_full(dve, g, o_job[lt])
                        dve.tensor_tensor(acc[:, lt, :], bank(o_job[lt]), acc[:, lt, :],
                                          ALU.add).then_inc(ring.freed(o_job[lt]), 1)
                    dve.drain()
                barrier(dve, done, b)

            add(sp_, pool_, pe_, act_, dve_)
            own.close()

        def wide(i_):
            tag, nth = "w", int(i_) - 1
            own = ExitStack()
            H, C = 16, 8
            SC = float(1.0 / np.sqrt(np.float32(P)))
            W = {"k": t["L2_xattn_wk" + i_], "q": t["L2_xattn_wq" + i_], "v": t["L2_xattn_wv" + i_],
                 "o": t["L2_xattn_wo" + i_]}
            c_bq, c_bk, c_xk, c_xv = (at[n + "_2" + i_] for n in ("bq", "bk", "xk", "xv"))
            raw = sb(own, tag + "_raw", [P, 2, 1024])
            w = {k: Pair(own, f"{tag}_w{k}", [P, KC, 256] if k != "o" else [P, 2, D]) for k in "kqvo"}
            kt, qt = Pair(own, tag + "_k", [P, 2, NK]), Pair(own, tag + "_q", [P, 2, NQ])
            vv = Pair(own, tag + "_v", [P, ST, 256])
            v32 = sb(own, tag + "_v32", [P, 2, 2, 256])
            prob = sb(own, tag + "_p", [P, 2, LT, NK])
            pt = Pair(own, tag + "_pt", [P, 4, NQ])
            att = Pair(own, tag + "_att", [P, NQ])
            vrow = sb(own, tag + "_vrow", [P, 2, 256])
            cv = sb(own, tag + "_cv", [P, 256])
            xk = Pair(own, tag + "_xk", [P, H, 2])
            xv = Pair(own, tag + "_xv", [P, 2])
            xl = sb(own, tag + "_xl", [P, 2, LT])
            crow = sb(own, tag + "_crow", [1, D])
            crow_p = Pair(own, tag + "_crowp", [1, D])
            mx, nm, z, ex, zx, rz = (sb(own, tag + n, [P, 2, LT]) for n in ("_mx", "_nm", "_z", "_ex", "_zx", "_rz"))

            plan, n = [], 0
            job = {}
            def ring_step(*x):
                nonlocal n
                job[x] = n
                plan.append(x)
                n += 1
            for x in (("k", 0, 0), ("k", 0, 1), ("q", 0), ("x", 0)):
                ring_step(*x)
            plan += [("s", 0, 0), ("s", 0, 1)]
            ring_step("k", 1, 0)
            plan.append(("s", 0, 2))
            ring_step("k", 1, 1)
            plan.append(("s", 0, 3))
            ring_step("q", 1)
            ring_step("x", 1)
            for v in range(4):
                ring_step("v", v)
            for u in range(2):
                def pv(v):
                    if v == 0:
                        nonlocal n
                        job["pv", u] = n
                        n += 1
                    plan.append(("pv", u, v))
                if u == 1:
                    plan += [("t", 1, 0), ("t", 1, 1)]
                    ring_step("c")
                    for lt in range(LT):
                        ring_step("o", 0, lt)
                for v in range(ST):
                    if u == 0 or v >= 2:
                        plan.append(("t", u, v))
                    if u == 0 and v % 2 == 1:
                        plan.append(("s", 1, v // 2))
                    if v >= 2:
                        pv(v - 2)
                pv(ST - 2)
                pv(ST - 1)
            for lt in range(LT):
                ring_step("o", 1, lt)

            ring = Slots(sem, tag + "_ring", 2, n)
            ring_hi = sem(tag + "_ring_hi")
            turn = Slots(sem, tag + "_turn", 2, 2 * ST)
            turn_hi = sem(tag + "_turn_hi")
            score = Slots(sem, tag + "_score", 2, 2 * LT)
            max_own, max_done = sem(tag + "_max_own"), sem(tag + "_max_done")
            extra_exp = sem(tag + "_extra_exp")
            v_hi, v_done = sem(tag + "_v_hi"), sem(tag + "_v_done")
            own_d = sem(tag + "_dve_own")
            loaded = {k: sem(f"{tag}_loaded_{k}") for k in "kqvo"}
            rows_loaded, crow_loaded = sem(tag + "_rows_loaded"), sem(tag + "_crow_loaded")
            cv_done, xv_done, xk_done = (sem(tag + x) for x in ("_cv_done", "_xv_done", "_xk_done"))
            split = {k: sem(f"{tag}_split_{k}") for k in "kqvo"}
            pool_hi = sem(tag + "_pool_hi")
            row_done, row_full = sem(tag + "_row_done"), sem(tag + "_row_full")
            last_use = {"k": job["k", 1, 1], "q": job["q", 1], "v": job["v", 3], "o": job["o", 1, 3]}
            credits.extend([ring, turn, score])
            extra_credits.extend(list(split.values()) + [cv_done])
            done = new_barrier()
            bank = lambda m: ps[:, R_BANK + m % 2, :]

            def view(name):
                if name == "o":
                    return W["o"].rearrange("(c k p) n -> c p k n", p=P, k=2)
                return W[name].rearrange("(k p) (c n) -> c p k n", p=P, n=256)

            def raw_of(i, name):
                return raw[:, i % 2, :].rearrange("p (k n) -> p k n", k=2 if name == "o" else KC)

            def sp_(sp, b):
                bb = b * 2 + nth
                sp.dma_start(crow[:, :], t["L2_xattn_bo" + i_].unsqueeze(0)).then_inc(crow_loaded, 16)
                with sp.Fori(0, C) as c:
                    g = bb * C + c
                    for i, name in enumerate("kqvo"):
                        sp.wait_ge(split["vokq"[i]], g + (1 if i < 2 else 2))
                        sp.dma_start(raw_of(i, name), view(name)[c, :, :, :]).then_inc(loaded[name], 16)
                        if i == 1:
                            sp.wait_ge(cv_done, g + 1)
                            for r, src in enumerate((t["L2_xattn_bv" + i_].rearrange("(c n) -> c n", n=256),
                                                     t["L2_xattn_bias_v" + i_].rearrange("a b (c h) k -> (a b c) (h k)", h=2))):
                                sp.dma_start(vrow[:, r, :], src[c, :].unsqueeze(0).broadcast_to([P, 256])
                                             ).then_inc(rows_loaded, 16)
                barrier(sp, done, b)

            def pool_(pool, b):
                bb = b * 2 + nth
                with pool.Fori(0, C) as c:
                    g = bb * C + c
                    for i, name in enumerate("kqvo"):
                        pool.wait_ge(loaded[name], g * 16 + 16)
                        ring.wait_full_before(pool, g, last_use[name])
                        hi, lo = w[name][:, :, :]
                        apart(pool)
                        pool.tensor_copy(hi, raw_of(i, name)).then_inc(pool_hi, 1)
                        pool.wait_ge(pool_hi, g * 4 + i + 1)
                        pool.tensor_tensor(lo, raw_of(i, name), as_f32(hi), ALU.subtract).then_inc(split[name], 1)
                barrier(pool, done, b)

            def pe_(pe, b):
                bb = b * 2 + nth
                pe.wait_ge(xk_done, bb + 1)
                apart(pe)
                with pe.Fori(0, C) as c:
                    g = bb * C + c
                    for x in plan:
                        m = job.get(x)
                        if x[0] in "kq" and x[-1] == 0 and x[1] == 0:
                            pe.wait_ge(split[x[0]], g + 2)
                        if x[0] == "k":
                            _, u, h = x
                            ring.wait_free(pe, g, m)
                            for k in range(KC):
                                i = mm3(pe, bank(m), w["k"][:, k, u * P:(u + 1) * P], CT[:, k, h * 512:(h + 1) * 512],
                                        k == 0, k == KC - 1)
                            i.then_inc(ring.full, 1)
                        elif x[0] == "q":
                            ring.wait_free(pe, g, m)
                            for k in range(KC):
                                i = mm3(pe, bank(m), w["q"][:, k, x[1] * P:(x[1] + 1) * P], XT[:, k, :],
                                        k == 0, k == KC - 1)
                            i.then_inc(ring.full, 1)
                        elif x[0] == "x":
                            u = x[1]
                            ring.wait_done(pe, g, job["q", u])
                            ring.wait_free(pe, g, m)
                            for lt in range(LT):
                                i = mm3(pe, bank(m)[:, 2 * lt:2 * lt + 2], qt[:, u, lt * P:(lt + 1) * P],
                                        (xk.h[:, bass.ds(c * 2 + u, 1), :], xk.l[:, bass.ds(c * 2 + u, 1), :]),
                                        lt == 0, True)
                            i.then_inc(ring.full, 1)
                        elif x[0] == "v":
                            if x[1] == 0:
                                pe.wait_ge(split["v"], g + 2)
                            ring.wait_free(pe, g, m)
                            for q in range(2):
                                for k in range(KC):
                                    i = mm3(pe, bank(m)[:, q * 256:(q + 1) * 256],
                                            CT[:, k, (2 * x[1] + q) * P:(2 * x[1] + q + 1) * P], w["v"][:, k, :],
                                            k == 0 and q == 0, k == KC - 1)
                            i.then_inc(ring.full, 1)
                        elif x[0] == "s":
                            _, u, lt = x
                            if lt == 0:
                                ring.wait_done(pe, g, job["k", u, 0])
                                ring.wait_done(pe, g, job["k", u, 1])
                            sn = u * LT + lt
                            score.wait_free(pe, g, sn)
                            for h in range(2):
                                i = mm3(pe, ps[:, S_BANK + 2 * (sn % 2) + h, :], qt[:, u, lt * P:(lt + 1) * P],
                                        kt[:, u, h * 512:(h + 1) * 512], True, True)
                            i.then_inc(score.full, 1)
                        elif x[0] == "t":
                            _, u, v = x
                            tn = u * ST + v
                            if v == 0:
                                score.wait_done(pe, g, u * LT + 2)
                                score.wait_done(pe, g, u * LT + 3)
                            turn.wait_free(pe, g, tn)
                            for lt in range(LT):
                                i = pe.transpose(ps[:, T_BANK + tn % 2, lt * P:(lt + 1) * P],
                                                 prob[:, u, lt, v * P:(v + 1) * P], ident[:, :])
                            i.then_inc(turn.full, 1)
                        elif x[0] == "pv":
                            _, u, v = x
                            tn, m = u * ST + v, job["pv", u]
                            if v == 0:
                                ring.wait_free(pe, g, m)
                                pe.wait_ge(v_done, g * 4 + 4)
                            turn.wait_done(pe, g, tn)
                            i = mm3(pe, bank(m), vv[:, v, u * P:(u + 1) * P], pt[:, tn % 4, :], v == 0, v == ST - 1)
                            if v == ST - 1:
                                i.then_inc(ring.full, 1)
                        elif x[0] == "c":
                            pe.wait_ge(split["o"], g + 2)
                            pe.wait_ge(xv_done, g + 1)
                            ring.wait_free(pe, g, m)
                            for h in range(2):
                                i = mm3(pe, bank(m)[0:1, :], xv[:, h:h + 1], w["o"][:, h, :], h == 0, h == 1)
                            i.then_inc(ring.full, 1)
                        else:
                            _, u, lt = x
                            if lt == 0:
                                ring.wait_done(pe, g, job["pv", u])
                            ring.wait_free(pe, g, m)
                            mm3(pe, bank(m), att[:, lt * P:(lt + 1) * P], w["o"][:, u, :], True,
                                True).then_inc(ring.full, 1)
                pe.wait_ge(row_done, bb + 1)
                pe.matmul(ps[:, S_BANK, :], ones_row[:, :], crow_p.h[:, :], start=True, stop=False)
                pe.matmul(ps[:, S_BANK, :], ones_row[:, :], crow_p.l[:, :], start=False, stop=True).then_inc(row_full, 1)
                barrier(pe, done, b)

            def act_(act, b):
                bb = b * 2 + nth
                with act.Fori(0, C) as c:
                    g = bb * C + c
                    for x in plan:
                        m = job.get(x)
                        if x[0] == "k":
                            _, u, h = x
                            ring.wait_full(act, g, m)
                            apart(act)
                            act.activation(kt.h[:, u, h * 512:(h + 1) * 512], bank(m), ACT.Identity,
                                           bias=cols[:, bass.ds(c * 2 + (c_bk + u), 1)]).then_inc(ring_hi, 1)
                        elif x[0] == "q":
                            ring.wait_full(act, g, m)
                            apart(act)
                            act.activation(qt.h[:, x[1], :], bank(m), ACT.Identity,
                                           bias=cols[:, bass.ds(c * 2 + (c_bq + x[1]), 1)]).then_inc(ring_hi, 1)
                        elif x[0] == "v":
                            ring.wait_done(act, g, m)
                            act.activation(vv.h[:, 2 * x[1]:2 * x[1] + 2, :], v32[:, x[1] % 2, :, :],
                                           ACT.Copy).then_inc(v_hi, 1)
                        elif x[0] == "s":
                            _, u, lt = x
                            sn = u * LT + lt
                            act.wait_ge(max_done, g * 2 * LT + sn + 1)
                            act.activation(ex[:, u, lt:lt + 1], xl[:, u, lt:lt + 1], ACT.Exp,
                                           bias=nm[:, u, lt:lt + 1], scale=SC)
                            act.activation(prob[:, u, lt, :].rearrange("p (h w) -> p h w", h=2),
                                           ps[:, S_BANK + 2 * (sn % 2):S_BANK + 2 * (sn % 2) + 2, :], ACT.Exp,
                                           bias=nm[:, u, lt:lt + 1], scale=SC,
                                           accum_out=z[:, u, lt:lt + 1]).then_inc(score.freed(sn), 1)
                        elif x[0] == "t":
                            tn = x[1] * ST + x[2]
                            turn.wait_full(act, g, tn)
                            act.activation(pt.h[:, tn % 4, :], ps[:, T_BANK + tn % 2, :], ACT.Copy).then_inc(turn_hi, 1)
                        elif x[0] == "pv" and x[2] == ST - 1:
                            ring.wait_full(act, g, job["pv", x[1]])
                            act.activation(att.h[:, :], bank(job["pv", x[1]]), ACT.Copy).then_inc(ring_hi, 1)
                barrier(act, done, b)

            def dve_(dve, b):
                bb = b * 2 + nth
                src = cols[:, c_xk:c_xk + H].unsqueeze(2).broadcast_to([P, H, 2])
                dve.tensor_copy(xk.h[:, :, :], src)
                dve.drain()
                dve.tensor_tensor(xk.l[:, :, :], src, as_f32(xk.h[:, :, :]), ALU.subtract).then_inc(xk_done, 1)
                dve.wait_ge(crow_loaded, bb * 16 + 16)
                apart(dve)
                with dve.Fori(0, C) as c:
                    g = bb * C + c
                    pair_xv = cols[:, bass.ds(c * 2 + c_xv, 2)]
                    dve.wait_ge(rows_loaded, g * 32 + 32)
                    dve.tensor_tensor(cv[:, :], vrow[:, 0, :], vrow[:, 1, :], ALU.subtract).then_inc(cv_done, 1)
                    dve.tensor_copy(xv.h[:, :], pair_xv)
                    dve.drain()
                    dve.tensor_tensor(xv.l[:, :], pair_xv, as_f32(xv.h[:, :]), ALU.subtract).then_inc(xv_done, 1)
                    n_hi = 0
                    for x in plan:
                        m = job.get(x)
                        if x[0] == "k":
                            _, u, h = x
                            n_hi += 1
                            dve.wait_ge(ring_hi, g * 8 + n_hi)
                            sl = slice(h * 512, (h + 1) * 512)
                            dve.scalar_tensor_tensor(out=kt.l[:, u, sl], in0=bank(m),
                                                     scalar=cols[:, bass.ds(c * 2 + (c_bk + u), 1)],
                                                     in1=as_f32(kt.h[:, u, sl]), op0=ALU.add,
                                                     op1=ALU.subtract).then_inc(ring.freed(m), 1)
                        elif x[0] == "q":
                            n_hi += 1
                            dve.wait_ge(ring_hi, g * 8 + n_hi)
                            dve.scalar_tensor_tensor(out=qt.l[:, x[1], :], in0=bank(m),
                                                     scalar=cols[:, bass.ds(c * 2 + (c_bq + x[1]), 1)],
                                                     in1=as_f32(qt.h[:, x[1], :]), op0=ALU.add,
                                                     op1=ALU.subtract).then_inc(ring.freed(m), 1)
                        elif x[0] == "x":
                            ring.wait_full(dve, g, m)
                            dve.tensor_copy(xl[:, x[1], :], bank(m)[:, 0:2 * LT].rearrange("p (l e) -> p l e", e=2)[:, :, 0]
                                            ).then_inc(ring.freed(m), 1)
                        elif x[0] == "v":
                            ring.wait_full(dve, g, m)
                            dve.tensor_tensor(v32[:, x[1] % 2, :, :], bank(m).rearrange("p (q w) -> p q w", q=2),
                                              cv[:, :].unsqueeze(1).broadcast_to([P, 2, 256]),
                                              ALU.add).then_inc(ring.freed(m), 1)
                            dve.wait_ge(v_hi, g * 4 + x[1] + 1)
                            dve.tensor_tensor(vv.l[:, 2 * x[1]:2 * x[1] + 2, :], v32[:, x[1] % 2, :, :],
                                              as_f32(vv.h[:, 2 * x[1]:2 * x[1] + 2, :]), ALU.subtract).then_inc(v_done, 1)
                        elif x[0] == "s":
                            _, u, lt = x
                            sn = u * LT + lt
                            score.wait_full(dve, g, sn)
                            dve.tensor_reduce(mx[:, u, lt:lt + 1],
                                              ps[:, S_BANK + 2 * (sn % 2):S_BANK + 2 * (sn % 2) + 2, :], AX.XY,
                                              ALU.max).then_inc(max_own, 1)
                            if lt == 0:
                                ring.wait_done(dve, g, job["x", u])
                            dve.wait_ge(max_own, g * 2 * LT + sn + 1)
                            dve.tensor_scalar(nm[:, u, lt:lt + 1], mx[:, u, lt:lt + 1], xl[:, u, lt:lt + 1], -SC,
                                              ALU.max, ALU.mult).then_inc(max_done, 1)
                        elif x[0] == "t":
                            tn = x[1] * ST + x[2]
                            dve.wait_ge(turn_hi, g * 2 * ST + tn + 1)
                            dve.tensor_tensor(pt.l[:, tn % 4, :], ps[:, T_BANK + tn % 2, :], as_f32(pt.h[:, tn % 4, :]),
                                              ALU.subtract).then_inc(turn.freed(tn), 1)
                        elif x[0] == "pv" and x[2] == ST - 1:
                            u = x[1]
                            score.wait_done(dve, g, u * LT + 3)
                            dve.tensor_tensor(zx[:, u, :], z[:, u, :], ex[:, u, :], ALU.add).then_inc(own_d, 1)
                            dve.wait_ge(own_d, g * 4 + 2 * u + 1)
                            dve.reciprocal(rz[:, u, :], zx[:, u, :]).then_inc(own_d, 1)
                            n_hi += 1
                            dve.wait_ge(ring_hi, g * 8 + n_hi)
                            dve.tensor_tensor(att.l[:, :], bank(job["pv", u]), as_f32(att.h[:, :]),
                                              ALU.subtract).then_inc(ring.freed(job["pv", u]), 1)
                            dve.wait_ge(own_d, g * 4 + 2 * u + 2)
                        elif x[0] == "c":
                            ring.wait_full(dve, g, m)
                            dve.tensor_tensor(crow[:, :], bank(m)[0:1, :], crow[:, :], ALU.add).then_inc(ring.freed(m), 1)
                        elif x[0] == "o":
                            _, u, lt = x
                            ring.wait_full(dve, g, m)
                            if u == 1:
                                ring.wait_done(dve, g, job["o", 0, lt])
                            dve.scalar_tensor_tensor(out=X[:, lt, :], in0=bank(m), scalar=rz[:, u, lt:lt + 1],
                                                     in1=X[:, lt, :], op0=ALU.mult,
                                                     op1=ALU.add).then_inc(ring.freed(m), 1)
                    dve.drain()
                dve.tensor_copy(crow_p.h[:, :], crow[:, :])
                dve.drain()
                dve.tensor_tensor(crow_p.l[:, :], crow[:, :], as_f32(crow_p.h[:, :]), ALU.subtract).then_inc(row_done, 1)
                dve.wait_ge(row_full, bb + 1)
                for lt in range(LT):
                    dve.tensor_tensor(X[:, lt, :], ps[:, S_BANK, :], X[:, lt, :], ALU.add)
                barrier(dve, done, b)

            add(sp_, pool_, pe_, act_, dve_)
            own.close()

        norms = [0, 0]

        def norm(tag, src, eps, c_scale, c_shift, rms=False, first=None):
            own = ExitStack()
            xn = sb(own, tag + "_xn", [P, LT, D])
            tmp = sb(own, tag + "_tmp", [P, 2, NQ])
            stats, mv = sb(own, tag + "_st", [P, LT, 6]), sb(own, tag + "_mv", [P, LT, 2])
            ve, sd, rs = (sb(own, tag + n, [P, LT]) for n in ("_ve", "_sd", "_rs"))
            gb = sb(own, tag + "_gb", [P, 2, D]) if first else None
            turn_n = Turn(xn, XT, scale=c_scale, shift=c_shift, tmp=tmp)
            rows_ld = sem(tag + "_rows_loaded") if first else None
            var_done, sqrt_done, xn_done = (sem(n) for n in ("var_done", "sqrt_done", "xn_done"))
            rounds = 2 if first else 1
            nth, round0 = norms[0], norms[1]
            norms[0] += 1
            norms[1] += rounds
            done = new_barrier()

            def sp_(sp, b):
                if first:
                    for i in range(2):
                        sp.dma_start(gb[:, i, :], first[i].unsqueeze(0).broadcast_to([P, D])).then_inc(rows_ld, 16)
                barrier(sp, done, b)

            def pool_(pool, b):
                barrier(pool, done, b)

            def pe_(pe, b):
                pe.wait_ge(xn_done, b * norms[0] + (nth + 1))
                turn_n.pe(pe, b)
                barrier(pe, done, b)

            def act_(act, b):
                for r in range(rounds):
                    act.wait_ge(var_done, b * norms[1] + (round0 + r + 1))
                    act.activation(sd[:, :], ve[:, :], ACT.Sqrt).then_inc(sqrt_done, 1)
                turn_n.act(act, b)
                barrier(act, done, b)

            def dve_(dve, b):
                for r in range(rounds):
                    e = first[2] if first and r == 0 else eps
                    if rms:
                        for lt in range(LT):
                            dve.tensor_tensor_reduce(xn[:, lt, :], src[:, lt, :], src[:, lt, :], 1.0, 0.0, ALU.mult,
                                                     ALU.add, ve[:, lt:lt + 1])
                        dve.drain()
                        dve.tensor_scalar(ve[:, :], ve[:, :], 1.0 / D, float(e), ALU.mult, ALU.add).then_inc(var_done, 1)
                    else:
                        for lt in range(LT):
                            dve.bn_stats(stats[:, lt, :], src[:, lt, :])
                        dve.drain()
                        for lt in range(LT):
                            dve.bn_aggr(mv[:, lt, :], stats[:, lt, :])
                        dve.drain()
                        dve.tensor_scalar(ve[:, :], mv[:, :, 1], float(e), None, ALU.add).then_inc(var_done, 1)
                    dve.wait_ge(sqrt_done, b * norms[1] + (round0 + r + 1))
                    dve.reciprocal(rs[:, :], sd[:, :])
                    dve.drain()
                    for lt in range(LT):
                        if rms:
                            dve.tensor_scalar(xn[:, lt, :], src[:, lt, :], rs[:, lt:lt + 1], None, ALU.mult)
                        else:
                            dve.tensor_scalar(xn[:, lt, :], src[:, lt, :], mv[:, lt, 0:1], rs[:, lt:lt + 1],
                                              ALU.subtract, ALU.mult)
                    if r < rounds - 1:
                        dve.drain()
                        dve.wait_ge(rows_ld, b * 32 + 32)
                        for lt in range(LT):
                            dve.tensor_tensor(xn[:, lt, :], xn[:, lt, :], gb[:, 0, :], ALU.mult)
                        dve.drain()
                        for lt in range(LT):
                            dve.tensor_tensor(src[:, lt, :], xn[:, lt, :], gb[:, 1, :], ALU.add)
                        dve.drain()
                dve.drain().then_inc(xn_done, 1)
                turn_n.dve(dve, b)
                barrier(dve, done, b)

            add(sp_, pool_, pe_, act_, dve_)
            own.close()

        def mlp(nth, func, w1, w2, c_b1, b2, last):
            tag = "mlp"
            own = ExitStack()
            C = F // P // 2
            raw1, raw2 = sb(own, tag + "_raw1", [P, 2, KC, P]), sb(own, tag + "_raw2", [P, 2, D])
            p1 = [Pair(own, f"{tag}_w1{i}", [P, KC, P]) for i in range(2)]
            p2 = [Pair(own, f"{tag}_w2{i}", [P, D]) for i in range(2)]
            g32 = sb(own, tag + "_g32", [P, 2, NQ])
            gp = Pair(own, tag + "_g", [P, 2, NQ])
            brow, browp = sb(own, tag + "_b2", [1, D]), Pair(own, tag + "_b2p", [1, D])
            res = sb(own, tag + "_res", [P, LT, D]) if last else X
            ring = Slots(sem, tag + "_ring", 2, 2)
            ld1, ld2 = ([sem(f"{tag}_w{w}_loaded{i}") for i in range(2)] for w in "12")
            sp1, sp2 = ([sem(f"{tag}_w{w}_split{i}") for i in range(2)] for w in "12")
            pool_hi, w2_hi, g_hi = sem(tag + "_pool_hi"), sem(tag + "_w2_hi"), sem(tag + "_g_hi")
            act_done, hid_done, prod_done = sem(tag + "_act_done"), sem(tag + "_hidden_done"), sem(tag + "_product_done")
            b_ld, b_done, sum_done, stored = (sem(tag + n) for n in ("_b2_loaded", "_b2_done", "_sum_done", "_stored"))
            credits.append(ring)
            extra_credits.extend(sp1 + sp2 + [prod_done])
            done = new_barrier()

            def sp_(sp, b):
                bb = b * 2 + nth
                sp.dma_start(brow[:, :], b2.unsqueeze(0)).then_inc(b_ld, 16)
                with sp.Fori(0, C) as c:
                    g = bb * C + c
                    for i in range(2):
                        sp.wait_ge(sp1[i], g + 1)
                        sp.dma_start(raw1[:, i, :, :], w1.rearrange("(k p) (c n) -> c p k n", p=P, n=P)[c * 2 + i, :, :, :]
                                     ).then_inc(ld1[i], 16)
                        sp.wait_ge(sp2[i], g + 1)
                        sp.dma_start(raw2[:, i, :], w2.rearrange("(c p) n -> c p n", p=P)[c * 2 + i, :, :]
                                     ).then_inc(ld2[i], 16)
                if last:
                    sp.wait_ge(sum_done, bb + 1)
                    sp.dma_start(out[b, :, :].rearrange("(r p) d -> p r d", p=P), res[:, :, :]).then_inc(stored, 16)
                    sp.wait_ge(stored, b * 16 + 16)
                barrier(sp, done, b)

            def pool_(pool, b):
                bb = b * 2 + nth
                with pool.Fori(0, C) as c:
                    g = bb * C + c
                    for i in range(2):
                        pool.wait_ge(ld1[i], g * 16 + 16)
                        ring.wait_full_before(pool, g, i)
                        apart(pool)
                        pool.tensor_copy(p1[i].h[:, :, :], raw1[:, i, :, :]).then_inc(pool_hi, 1)
                        pool.wait_ge(pool_hi, g * 2 + i + 1)
                        pool.tensor_tensor(p1[i].l[:, :, :], raw1[:, i, :, :], as_f32(p1[i].h[:, :, :]),
                                           ALU.subtract).then_inc(sp1[i], 1)
                barrier(pool, done, b)

            def pe_(pe, b):
                bb = b * 2 + nth
                pe.wait_ge(b_done, bb + 1)
                for lt in range(LT):
                    pe.matmul(ps[:, lt, :], ones_row[:, :], browp.h[:, :], start=True, stop=False, skip_group_check=True)
                    pe.matmul(ps[:, lt, :], ones_row[:, :], browp.l[:, :], start=False, stop=False,
                              skip_group_check=True)
                with pe.Fori(0, C) as c:
                    g = bb * C + c
                    for i in range(2):
                        pe.wait_ge(sp1[i], g + 2)
                        ring.wait_free(pe, g, i)
                        for k in range(KC):
                            j = mm3(pe, ps[:, R_BANK + i, :], p1[i][:, k, :], XT[:, k, :], k == 0, k == KC - 1)
                        j.then_inc(ring.full, 1)
                    for i in range(2):
                        pe.wait_ge(sp2[i], g + 2)
                        pe.wait_ge(hid_done, g * 2 + i + 1)
                        for lt in range(LT):
                            j = mm3(pe, ps[:, lt, :], gp[:, i, lt * P:(lt + 1) * P], p2[i][:, :], False, False)
                        j.then_inc(prod_done, 1)
                barrier(pe, done, b)

            def act_(act, b):
                bb = b * 2 + nth
                with act.Fori(0, C) as c:
                    g = bb * C + c
                    for i in range(2):
                        ring.wait_full(act, g, i)
                        act.wait_ge(prod_done, g * 2 + i + 1)
                        apart(act)
                        act.activation(g32[:, i, :], ps[:, R_BANK + i, :], func,
                                       bias=cols[:, bass.ds(c * 2 + (c_b1 + i), 1)]).then_inc(ring.freed(i), 1)
                barrier(act, done, b)

            def dve_(dve, b):
                bb = b * 2 + nth
                dve.wait_ge(b_ld, bb * 16 + 16)
                dve.tensor_copy(browp.h[:, :], brow[:, :])
                dve.drain()
                dve.tensor_tensor(browp.l[:, :], brow[:, :], as_f32(browp.h[:, :]), ALU.subtract).then_inc(b_done, 1)
                with dve.Fori(0, C) as c:
                    g = bb * C + c
                    for i in range(2):
                        dve.wait_ge(ld2[i], g * 16 + 16)
                        dve.wait_ge(prod_done, g * 2 + i + 1)
                        dve.tensor_copy(p2[i].h[:, :], raw2[:, i, :]).then_inc(w2_hi, 1)
                        dve.wait_ge(w2_hi, g * 2 + i + 1)
                        dve.tensor_tensor(p2[i].l[:, :], raw2[:, i, :], as_f32(p2[i].h[:, :]),
                                          ALU.subtract).then_inc(sp2[i], 1)
                    for i in range(2):
                        ring.wait_done(dve, g, i)
                        dve.tensor_copy(gp.h[:, i, :], g32[:, i, :]).then_inc(g_hi, 1)
                        dve.wait_ge(g_hi, g * 2 + i + 1)
                        dve.tensor_tensor(gp.l[:, i, :], g32[:, i, :], as_f32(gp.h[:, i, :]),
                                          ALU.subtract).then_inc(hid_done, 1)
                dve.wait_ge(prod_done, bb * (2 * C) + (2 * C + 2))
                for lt in range(LT):
                    dve.tensor_tensor(res[:, lt, :], ps[:, lt, :], X[:, lt, :], ALU.add)
                dve.drain().then_inc(sum_done, 1)
                barrier(dve, done, b)

            add(sp_, pool_, pe_, act_, dve_)
            own.close()

        turn_1 = Turn(X, XT)
        bar = new_barrier()

        def turn_stage(turner, s):
            def sp_(sp, b):
                barrier(sp, s, b)

            def pool_(pool, b):
                barrier(pool, s, b)

            def pe_(pe, b):
                turner.pe(pe, b)
                barrier(pe, s, b)

            def act_(act, b):
                turner.act(act, b)
                barrier(act, s, b)

            def dve_(dve, b):
                turner.dve(dve, b)
                barrier(dve, s, b)

            add(sp_, pool_, pe_, act_, dve_)

        turn_stage(turn_1, bar)
        narrow("l1", X, 16, 4, NK, 0.25, at["bq_1"], at["bk_1"], at["bv_1"], t["L1_xattn_Wq"], t["L1_xattn_Wk"],
               t["L1_xattn_Wv"], t["L1_xattn_Wo"], t["L1_xattn_bo"], True)
        norm("n1", X, 1e-5, at["lns_1"], at["lno_1"], first=(t["L1_xattn_gamma"], t["L1_xattn_beta"], 1e-6))
        wide("1")
        norm("n2", X, 1e-5, at["lns_2"], at["lno_2"])
        wide("2")
        norm("n3", X, 1e-5, at["lns_m"], at["lno_m"])
        mlp(0, ACT.Gelu, t["L2_xattn_w_fc1"], t["L2_xattn_w_fc2"], at["b1_2"], t["L2_xattn_b_fc2"], False)
        turn_3 = Turn(X, XT)
        turn_stage(turn_3, new_barrier())
        l3 = ExitStack()
        acc3 = sb(l3, "acc3", [P, LT, D])
        narrow("l3", acc3, 32, 1, NK + NQ, 1.0 / 32, at["qb_3"], at["kb_3"], at["vb_3"], t["L3_xattn_q_w"],
               t["L3_xattn_kv_w"], None, t["L3_xattn_out_w"], t["L3_xattn_out_b"], False)
        norm("n4", acc3, 1e-6, at["pn_3"], None, rms=True)
        l3.close()
        mlp(1, ACT.Gelu_apprx_tanh, t["L3_xattn_mlp_w1"], t["L3_xattn_mlp_w2"], at["b1_3"], t["L3_xattn_mlp_b2"], True)

        pre = ExitStack()
        vec = sb(pre, "vec", [P, n_vt, P])
        pre.close()
        vec_clear = sem("vec_clear")

        def before_sp(sp):
            sp.wait_ge(vec_clear, 1)
            for r0_, n_, c_, w_, src in vec_rows:
                sp.dma_start(vec[r0_ % P:r0_ % P + n_, r0_ // P, c_:c_ + w_], src,
                             allow_slow_non_contiguous=src.ap[-1][0] != 1).then_inc(s_vec, 16)
            sp.dma_start(alpha[:, :], t["L0_xattn_alpha"].unsqueeze(0).broadcast_to([P, 1])).then_inc(s_vec, 16)

        def before_pool(pool):
            pool.memset(vec[:, :, :], 0.0).then_inc(vec_clear, 1)
            pool.memset(ident[:, :], 0.0).then_inc(s_pool, 1)
            pool.wait_ge(s_pool, 1)
            pool.affine_select(out=ident[:, :], in_=ident[:, :], compare_op=ALU.not_equal, fill=1.0, base=0,
                               pattern=[[-1, P]], channel_multiplier=1).then_inc(s_const, 1)
            pool.memset(zero_col[:, :], 0.0).then_inc(s_const, 1)
            pool.memset(as_f32(ones_row[:, :]), 1.0).then_inc(s_const, 1)

        def before_pe(pe):
            for ring_ in {r.full.name: r for r in credits}.values():
                ring_.credit(pe)
            for s in {s.name: s for s in extra_credits}.values():
                pe.sem_inc(s, 1)
            pe.sem_inc(sems["mlp_product_done"], 1)
            pe.wait_ge(s_const, 3)
            pe.wait_ge(s_vec, 16 * (len(vec_rows) + 1))
            for i in range(n_vt):
                m = pe.transpose(ps[:, 0, i * P:(i + 1) * P], vec[:, i, :], ident[:, :])
            m.then_inc(s_vt, 1)

        def before_dve(dve):
            dve.wait_ge(s_vt, 1)
            dve.tensor_copy(cols[:, :], ps[:, 0, 0:n_vt * P]).then_inc(s_cols, 1)

        block = ctx.enter_context(nc.Block())

        def all_stages(eng, name):
            eng.wait_ge(s_cols, 1)
            with eng.Fori(0, B) as b:
                for st in stages:
                    st[name](eng, b)

        @block.sync
        def _(sp):
            before_sp(sp)
            all_stages(sp, "sp")

        @block.gpsimd
        def _(pool):
            before_pool(pool)
            all_stages(pool, "pool")

        @block.tensor
        def _(pe):
            before_pe(pe)
            all_stages(pe, "pe")

        @block.scalar
        def _(act):
            all_stages(act, "act")

        @block.vector
        def _(dve):
            before_dve(dve)
            all_stages(dve, "dve")


def kernel(**inputs):
    import concourse.bacc as bacc
    from concourse.bass_utils import run_bass_kernel_spmd

    nc = bacc.Bacc("TRN2", target_bir_lowering=False, num_devices=1)
    arrays, t = {}, {}
    for name, value in inputs.items():
        a = np.ascontiguousarray(value).reshape(np.shape(value) or (1,))
        arrays["in_" + name] = a
        t[name] = nc.dram_tensor("in_" + name, a.shape, mybir.dt.from_np(a.dtype), kind="ExternalInput").ap()
    out = nc.dram_tensor("out_0", (B, NQ, D), F32, kind="ExternalOutput").ap()
    build(nc, t, out)
    r = run_bass_kernel_spmd(nc, [arrays], core_ids=[0])
    return r.results[0]["out_0"]
```

```python
from contextlib import ExitStack

import numpy as np
import concourse.bass as bass
from concourse import mybir

F32 = mybir.dt.float32
F32R = mybir.dt.float32r
I32 = mybir.dt.int32
ACT = mybir.ActivationFunctionType
ALU = mybir.AluOpType
AX = mybir.AxisListType

P = 128
B = 2
NQ = 512
NK = 1024
D = 512
KC = D // P
LT = NQ // P
ST = NK // P
F = 2048
BLOCKED = -3.0e38
ENGINES = 5


TOUCHED = []


def apart(eng):
    eng.sem_inc(TOUCHED[0], 1)


class Slots:

    def __init__(self, sem, name, slots, jobs, mixed=False):
        self.slots, self.jobs, self.mixed = slots, jobs, mixed
        self.full = sem(name + "_full")
        self.free = [sem(f"{name}_free{s}") for s in range(slots)] if mixed else [sem(name + "_free")]
        self.per = [len(range(s, jobs, slots)) for s in range(slots)]

    def credit(self, eng):
        for f in self.free:
            eng.sem_inc(f, 1 if self.mixed else self.slots)
        eng.sem_inc(self.full, self.jobs)

    def _wait(self, eng, g, counts):
        for s in sorted({s for s, _ in counts}):
            per_pass = self.per[s] if self.mixed else self.jobs
            eng.wait_ge(self.free[s], g * per_pass + max(v for c, v in counts if c == s))

    def _free(self, n):
        s = n % self.slots
        if self.mixed:
            return s, n // self.slots + 1
        before = n - self.slots
        if before < 0 and self.jobs % self.slots:
            before = (self.per[s] - 1) * self.slots + s - self.jobs
        return 0, before + 1 + self.slots

    def _done(self, n):
        return (n % self.slots, n // self.slots + 2) if self.mixed else (0, n + 1 + self.slots)

    def wait_free(self, eng, g, n, done=()):
        self._wait(eng, g, [self._free(n)] + [self._done(m) for m in done])

    def wait_done(self, eng, g, *done):
        self._wait(eng, g, [self._done(m) for m in done])

    def wait_full(self, eng, g, n):
        eng.wait_ge(self.full, g * self.jobs + (self.jobs + n + 1))

    def wait_full_before(self, eng, g, n):
        eng.wait_ge(self.full, g * self.jobs + (n + 1))

    def freed(self, n):
        return self.free[n % self.slots] if self.mixed else self.free[0]


def build(nc, t, out):
    ctx = ExitStack()
    sems = {}

    def sem(name):
        if name not in sems:
            sems[name] = ctx.enter_context(nc.semaphore(name))
        return sems[name]

    with ctx:
        uid = [0]

        def sb(stack, name, shape, dt=F32):
            uid[0] += 1
            return stack.enter_context(nc.sbuf_tensor(f"{name}_{uid[0]}", shape, dt))

        class Pair:

            def __init__(self, stack, name, shape):
                self.h = sb(stack, name + "_hi", shape, F32R)
                self.l = sb(stack, name + "_lo", shape, F32R)

            def __getitem__(self, key):
                return self.h[key], self.l[key]

        class View:

            def __init__(self, hi, lo):
                self.h, self.l = hi, lo

            def __getitem__(self, key):
                return self.h[key], self.l[key]

        def mm3(pe, o, a, b, start, stop):
            pe.matmul(o, a[0], b[0], start=start, stop=False, skip_group_check=True)
            pe.matmul(o, a[0], b[1], start=False, stop=False, skip_group_check=True)
            return pe.matmul(o, a[1], b[0], start=False, stop=stop, skip_group_check=True)

        def as_f32(ap):
            return ap.bitcast(F32)

        ps = ctx.enter_context(nc.psum_tensor("ps", [P, 8, 512], F32))
        S_BANK, T_BANK, R_BANK = 0, 4, 6

        ident = sb(ctx, "ident", [P, P])
        X = sb(ctx, "X", [P, LT, D])
        XT = Pair(ctx, "XT", [P, KC, NQ])
        CT = Pair(ctx, "CT", [P, KC, NK])
        ones_row = sb(ctx, "ones_row", [1, P], F32R)
        ones_32 = sb(ctx, "ones_32", [P, 32])
        ident_r = sb(ctx, "ident_r", [P, P], F32R)
        zero_col = sb(ctx, "zero_col", [P, 1])
        alpha = sb(ctx, "alpha", [P, 1])

        vec_rows = []
        at = {}
        n_rows = [0]

        def column(name, src):
            n, w = src.shape
            if n_rows[0] % P + n > P:
                n_rows[0] += P - n_rows[0] % P
            at[name] = n_rows[0]
            vec_rows.append((n_rows[0], n, 0, w, src))
            n_rows[0] += n

        def chunked(name, w=P):
            return t[name].rearrange("(c p) -> c p", p=w)

        column("bq_1", chunked("L1_xattn_bq"))
        column("bk_1", chunked("L1_xattn_bk", 32))
        at["bv_1"] = n_rows[0]
        for rep in range(4):
            vec_rows.append((n_rows[0], 8, rep * 32, 16, t["L1_xattn_bv"].rearrange("(g d) -> g d", g=8)))
        n_rows[0] += 8
        for i in "12":
            column("lns_" + i, chunked(f"L2_xattn_ln{i}_scale"))
            column("lno_" + i, chunked(f"L2_xattn_ln{i}_offset"))
        column("lns_m", chunked("L2_xattn_ln_mlp_scale"))
        column("lno_m", chunked("L2_xattn_ln_mlp_offset"))
        column("b1_2", chunked("L2_xattn_b_fc1"))
        column("b1_3", chunked("L3_xattn_mlp_b1"))
        column("qb_3", chunked("L3_xattn_q_b"))
        kvb = t["L3_xattn_kv_b"].rearrange("(c p two) -> two c p", p=P, two=2)
        column("kb_3", kvb[0])
        column("vb_3", kvb[1])
        column("pn_3", chunked("L3_xattn_postnorm_w"))
        for i in "12":
            column("bq_2" + i, chunked(f"L2_xattn_bq{i}"))
            column("bk_2" + i, chunked(f"L2_xattn_bk{i}"))
            column("xk_2" + i, t[f"L2_xattn_bias_k{i}"].rearrange("a b h k -> (a b h) k"))
            column("xv_2" + i, t[f"L2_xattn_bias_v{i}"].rearrange("a b h k -> (a b h) k"))
        n_vt = -(-n_rows[0] // P)
        cols = sb(ctx, "cols", [P, n_vt * P])

        s_vec = sem("vectors_loaded")
        s_const = sem("constants_made")
        s_pool = sem("pool_own")
        s_vt = sem("vectors_turned")
        s_cols = sem("columns_ready")
        TOUCHED[:] = [sem("touched")]

        n_stage = [0]
        stage_done = sem("stage_done")

        def new_barrier():
            n_stage[0] += 1
            return n_stage[0]

        def barrier(eng, s, b):
            apart(eng)
            eng.drain().then_inc(stage_done, 1)
            eng.wait_ge(stage_done, b * (n_stage[0] * ENGINES) + s * ENGINES)
            apart(eng)

        credits = []
        extra_credits = []
        deep_credits = {}
        stages = []

        def add(sp, pool, pe, act, dve):
            stages.append({"sp": sp, "pool": pool, "pe": pe, "act": act, "dve": dve})

        class Turn:
            turns = {1: 0, 2: 0}

            def __init__(self, src, dst, halves=1, scale=None, shift=None, tmp=None):
                name = f"turn{halves}"
                self.halves, self.nth = halves, Turn.turns[halves]
                Turn.turns[halves] += 1
                self.src, self.dst, self.scale, self.shift, self.tmp = src, dst, scale, shift, tmp
                self.jobs = [(c, h) for h in range(halves) for c in range(KC)]
                self.ring = Slots(sem, name, 2, len(self.jobs))
                self.hi = sem(name + "_hi_done")
                credits.append(self.ring)

            def round_of(self, b):
                return b * Turn.turns[self.halves] + self.nth

            def pe(self, pe, b):
                b = self.round_of(b)
                for n, (c, h) in enumerate(self.jobs):
                    self.ring.wait_free(pe, b, n)
                    for r in range(4):
                        i = pe.transpose(ps[:, T_BANK + n % 2, r * P:(r + 1) * P],
                                         self.src[:, 4 * h + r, c * P:(c + 1) * P], ident[:, :])
                    i.then_inc(self.ring.full, 1)

            def act(self, act, b):
                b = self.round_of(b)
                for n, (c, h) in enumerate(self.jobs):
                    self.ring.wait_full(act, b, n)
                    bank = ps[:, T_BANK + n % 2, :]
                    hi = self.dst.h[:, c, h * 512:(h + 1) * 512]
                    if self.scale is None:
                        act.activation(hi, bank, ACT.Copy).then_inc(self.hi, 1)
                        continue
                    sc = cols[:, self.scale + c:self.scale + c + 1]
                    sh = zero_col[:, :] if self.shift is None else cols[:, self.shift + c:self.shift + c + 1]
                    act.activation(self.tmp[:, n % 2, :], bank, ACT.Identity, bias=sh, scale=sc)
                    act.activation(hi, bank, ACT.Identity, bias=sh, scale=sc).then_inc(self.hi, 1)

            def dve(self, dve, b):
                b = self.round_of(b)
                for n, (c, h) in enumerate(self.jobs):
                    dve.wait_ge(self.hi, b * len(self.jobs) + n + 1)
                    src = ps[:, T_BANK + n % 2, :] if self.scale is None else self.tmp[:, n % 2, :]
                    hi = self.dst.h[:, c, h * 512:(h + 1) * 512]
                    lo = self.dst.l[:, c, h * 512:(h + 1) * 512]
                    dve.tensor_tensor(lo, src, as_f32(hi), ALU.subtract).then_inc(self.ring.freed(n), 1)

        l0 = ExitStack()
        ctx_nat = sb(l0, "ctx_nat", [P, ST, D])
        s_x = sem("x_loaded")
        s_ctx = [sem(f"ctx_loaded{h}") for h in range(2)]
        turn_x = Turn(X, XT)
        turn_c = Turn(ctx_nat, CT, halves=2)
        bar = new_barrier()

        def load_sp(sp, b, s=bar):
            sp.dma_start(X[:, :, :], t["x"][b, :, :].rearrange("(r p) d -> p r d", p=P)).then_inc(s_x, 16)
            c = t["ctx_2048"][b, :, :].rearrange("(h r p) d -> h p r d", p=P, h=2)
            for h in range(2):
                sp.dma_start(ctx_nat[:, 4 * h:4 * h + 4, :], c[h]).then_inc(s_ctx[h], 16)
            barrier(sp, s, b)

        def load_pe(pe, b, s=bar):
            pe.wait_ge(s_x, b * 16 + 16)
            turn_x.pe(pe, b)
            for h in range(2):
                pe.wait_ge(s_ctx[h], b * 16 + 16)
            turn_x.ring.wait_done(pe, turn_x.round_of(b), 2, 3)
            turn_c.pe(pe, b)
            barrier(pe, s, b)

        def load_act(act, b, s=bar):
            turn_x.act(act, b)
            turn_c.act(act, b)
            barrier(act, s, b)

        def load_dve(dve, b, s=bar):
            turn_x.dve(dve, b)
            turn_c.dve(dve, b)
            barrier(dve, s, b)

        def load_pool(pool, b, s=bar):
            barrier(pool, s, b)

        add(load_sp, load_pool, load_pe, load_act, load_dve)

        w_nat = sb(l0, "l0_w", [P, 2, KC, D])
        wa = Pair(l0, "l0_wa", [P, KC, D])
        wb = Pair(l0, "l0_wb", [P, KC, D])
        gq = Pair(l0, "l0_g", [P, KC, D])
        yt = Pair(l0, "l0_y", [P, KC, NQ])
        cn = Pair(l0, "l0_cn", [P, 2, D])
        l0_p = sb(l0, "l0_p", [P, LT, NK])
        l0_pt = Pair(l0, "l0_pt", [P, 2, NQ])
        l0_mx = sb(l0, "l0_mx", [P, LT])
        l0_nm = sb(l0, "l0_nm", [P, LT])
        l0_z = sb(l0, "l0_z", [P, LT])
        l0_r = sb(l0, "l0_r", [P, LT])
        l0_ra = sb(l0, "l0_ra", [P, LT])
        SC0 = float(1.0 / np.sqrt(np.float32(D)))
        w0 = [sem(f"l0_w_loaded{i}") for i in range(4)]
        w0s = sem("l0_w_split")
        r0 = Slots(sem, "l0_ring", 2, 16)
        r0h = sem("l0_ring_hi")
        wt0 = Slots(sem, "l0_turn_wo", 2, 4)
        wt0h = sem("l0_turn_wo_hi")
        t0 = Slots(sem, "l0_turn_p", 2, ST)
        t0h = sem("l0_turn_p_hi")
        pv0 = sem("l0_pv_tile")
        s0 = Slots(sem, "l0_s", 2, LT)
        m0 = sem("l0_max")
        d0 = sem("l0_dve_own")
        cn0 = sem("l0_cn_split")
        cn0h = sem("l0_cn_hi")
        c0h = sem("l0_ctx_hi")
        c0l = sem("l0_ctx_split")
        credits += [r0, wt0, t0, s0]
        bar = new_barrier()
        W0 = ["L0_xattn_w_q", "L0_xattn_w_k", "L0_xattn_w_v", "L0_xattn_w_o"]

        def l0_sp(sp, b, s=bar):
            for i, name in enumerate(W0):
                if i == 2:
                    sp.wait_ge(w0s, b * 3 + 1)
                if i == 3:
                    sp.wait_ge(w0s, b * 3 + 2)
                sp.dma_start(w_nat[:, i % 2, :, :], t[name].rearrange("(c p) n -> p c n", p=P)).then_inc(w0[i], 16)
            barrier(sp, s, b)

        def l0_pool(pool, b, s=bar):
            for i, dst in enumerate((wa, wb, wa)):
                pool.wait_ge(w0[i], b * 16 + 16)
                if i == 2:
                    r0.wait_full(pool, b, 3)
                apart(pool)
                pool.tensor_copy(dst.h[:, :, :], w_nat[:, i % 2, :, :])
                pool.drain()
                pool.tensor_tensor(dst.l[:, :, :], w_nat[:, i % 2, :, :], as_f32(dst.h[:, :, :]),
                                   ALU.subtract).then_inc(w0s, 1)
            barrier(pool, s, b)

        def l0_pe(pe, b, s=bar):
            pe.wait_ge(w0s, b * 3 + 2)
            def chunk_jobs(n0, dst_cols, a, bb):
                for m in range(4):
                    n = n0 + m
                    r0.wait_free(pe, b, n)
                    for k in range(KC):
                        i = mm3(pe, ps[:, R_BANK + n % 2, :], a[:, k, m * P:(m + 1) * P], bb[:, k, :],
                                k == 0, k == KC - 1)
                    i.then_inc(r0.full, 1)
                return i
            chunk_jobs(0, None, wa, wb)
            r0.wait_done(pe, b, 2, 3)
            pe.wait_ge(w0[3], b * 16 + 16)
            for n in range(4):
                wt0.wait_free(pe, b, n)
                for r in range(4):
                    i = pe.transpose(ps[:, T_BANK + n % 2, r * P:(r + 1) * P],
                                     w_nat[:, 1, r, n * P:(n + 1) * P], ident[:, :])
                i.then_inc(wt0.full, 1)
            chunk_jobs(4, None, gq, XT)
            r0.wait_done(pe, b, 6, 7)
            for lt in range(LT):
                s0.wait_free(pe, b, lt)
                for hf in range(2):
                    for k in range(KC):
                        i = mm3(pe, ps[:, S_BANK + 2 * (lt % 2) + hf, :], yt[:, k, lt * P:(lt + 1) * P],
                                CT[:, k, hf * 512:(hf + 1) * 512], k == 0, k == KC - 1)
                i.then_inc(s0.full, 1)
            pe.wait_ge(w0s, b * 3 + 3)
            wt0.wait_done(pe, b, 2, 3)
            chunk_jobs(8, None, wa, wb)
            s0.wait_done(pe, b, LT - 2, LT - 1)
            for st in range(ST + 1):
                if st < ST:
                    t0.wait_free(pe, b, st)
                    for lt in range(LT):
                        i = pe.transpose(ps[:, T_BANK + st % 2, lt * P:(lt + 1) * P],
                                         l0_p[:, lt, st * P:(st + 1) * P], ident[:, :])
                    i.then_inc(t0.full, 1)
                if st:
                    v = st - 1
                    t0.wait_done(pe, b, v)
                    pe.wait_ge(cn0, b * ST + v + 1)
                    for m in range(4):
                        i = mm3(pe, ps[:, S_BANK + m, :], cn[:, v % 2, m * P:(m + 1) * P],
                                l0_pt[:, v % 2, :], v == 0, v == ST - 1)
                    i.then_inc(pv0, 1)
            pe.wait_ge(c0l, b * 4 + 4)
            r0.wait_done(pe, b, 10, 11)
            for lt in range(LT):
                n = 12 + lt
                r0.wait_free(pe, b, n)
                for k in range(KC):
                    i = mm3(pe, ps[:, R_BANK + n % 2, :], yt[:, k, lt * P:(lt + 1) * P], gq[:, k, :],
                            k == 0, k == KC - 1)
                i.then_inc(r0.full, 1)
            barrier(pe, s, b)

        def l0_act(act, b, s=bar):
            def split(n, dst, m):
                r0.wait_full(act, b, n)
                act.activation(dst.h[:, m, :], ps[:, R_BANK + n % 2, :], ACT.Copy).then_inc(r0h, 1)
            for m in range(4):
                split(m, gq, m)
            for n in range(4):
                wt0.wait_full(act, b, n)
                act.activation(wb.h[:, n, :], ps[:, T_BANK + n % 2, :], ACT.Copy).then_inc(wt0h, 1)
            for m in range(4):
                split(4 + m, yt, m)
            for lt in range(LT):
                act.wait_ge(m0, b * LT + lt + 1)
                act.activation(l0_p[:, lt, :], ps[:, S_BANK + 2 * (lt % 2):S_BANK + 2 * (lt % 2) + 2, :], ACT.Exp,
                               bias=l0_nm[:, lt:lt + 1], scale=SC0,
                               accum_out=l0_z[:, lt:lt + 1]).then_inc(s0.freed(lt), 1)
            for m in range(4):
                split(8 + m, gq, m)
            for st in range(ST):
                if st >= 2:
                    act.wait_ge(pv0, b * ST + st - 1)
                act.activation(cn.h[:, st % 2, :], ctx_nat[:, st, :], ACT.Copy).then_inc(cn0h, 1)
                t0.wait_full(act, b, st)
                act.activation(l0_pt.h[:, st % 2, :], ps[:, T_BANK + st % 2, :], ACT.Copy).then_inc(t0h, 1)
            act.wait_ge(pv0, b * ST + ST)
            for m in range(4):
                act.activation(yt.h[:, m, :], ps[:, S_BANK + m, :], ACT.Copy).then_inc(c0h, 1)
            barrier(act, s, b)

        def l0_dve(dve, b, s=bar):
            def lo(n, dst, m):
                dve.wait_ge(r0h, b * 12 + n + 1)
                dve.tensor_tensor(dst.l[:, m, :], ps[:, R_BANK + n % 2, :], as_f32(dst.h[:, m, :]),
                                  ALU.subtract).then_inc(r0.freed(n), 1)
            for m in range(4):
                lo(m, gq, m)
            for n in range(4):
                dve.wait_ge(wt0h, b * 4 + n + 1)
                dve.tensor_tensor(wb.l[:, n, :], ps[:, T_BANK + n % 2, :], as_f32(wb.h[:, n, :]),
                                  ALU.subtract).then_inc(wt0.freed(n), 1)
            for m in range(4):
                lo(4 + m, yt, m)
            for lt in range(LT):
                s0.wait_full(dve, b, lt)
                dve.tensor_reduce(l0_mx[:, lt:lt + 1], ps[:, S_BANK + 2 * (lt % 2):S_BANK + 2 * (lt % 2) + 2, :],
                                  AX.XY, ALU.max).then_inc(d0, 1)
                dve.wait_ge(d0, b * LT + lt + 1)
                dve.tensor_scalar(l0_nm[:, lt:lt + 1], l0_mx[:, lt:lt + 1], -SC0, None, ALU.mult).then_inc(m0, 1)
            for m in range(4):
                lo(8 + m, gq, m)
            for st in range(ST):
                dve.wait_ge(cn0h, b * ST + st + 1)
                dve.tensor_tensor(cn.l[:, st % 2, :], ctx_nat[:, st, :], as_f32(cn.h[:, st % 2, :]),
                                  ALU.subtract).then_inc(cn0, 1)
                dve.wait_ge(t0h, b * ST + st + 1)
                dve.tensor_tensor(l0_pt.l[:, st % 2, :], ps[:, T_BANK + st % 2, :], as_f32(l0_pt.h[:, st % 2, :]),
                                  ALU.subtract).then_inc(t0.freed(st), 1)
            for m in range(4):
                dve.wait_ge(c0h, b * 4 + m + 1)
                dve.tensor_tensor(yt.l[:, m, :], ps[:, S_BANK + m, :], as_f32(yt.h[:, m, :]),
                                  ALU.subtract).then_inc(c0l, 1)
            dve.reciprocal(l0_r[:, :], l0_z[:, :])
            dve.drain()
            dve.tensor_scalar(l0_ra[:, :], l0_r[:, :], alpha[:, 0:1], None, ALU.mult)
            dve.drain()
            for lt in range(LT):
                n = 12 + lt
                r0.wait_full(dve, b, n)
                dve.scalar_tensor_tensor(out=X[:, lt, :], in0=ps[:, R_BANK + n % 2, :], scalar=l0_ra[:, lt:lt + 1],
                                         in1=X[:, lt, :], op0=ALU.mult, op1=ALU.add).then_inc(r0.freed(n), 1)
            barrier(dve, s, b)

        add(l0_sp, l0_pool, l0_pe, l0_act, l0_dve)
        l0.close()

        def narrow(tag, acc, dh, rep, keys, scale, c_bq, c_bk, c_bv, w_q, w_k, w_v, w_o, bo, row_mask):
            own = ExitStack()
            C = D // P
            heads = P // dh
            kw = P // rep
            two = dh == 16
            groups, NS = heads // 4, 4
            n_ks = 1 if two else NS
            n_kv = kw // dh
            n_st, n_hf = keys // P, keys // 512
            s_slots = 6 // n_hf
            KS, KM = 3 * dh, 3 * dh + 2
            T = groups * n_st
            ZG = 4
            order = [u // 2 + (u % 2) * 4 for u in range(heads)] if two else list(range(heads))
            base = lambda u: 64 * (u // 4) if two else 0
            stack = lambda u: u % 4
            kv_of = lambda u: u // rep

            wk, wv = (Pair(own, tag + n, [P, KC, kw]) for n in ("_wk", "_wv"))
            wq, wo = Pair(own, tag + "_wq", [P, KC, P]), Pair(own, tag + "_wo", [P, groups, D])
            raw_q, raw_o = sb(own, tag + "_raw_q", [P, KC, P]), sb(own, tag + "_raw_o", [P, groups, D])
            raw_kv = sb(own, tag + "_raw_kv", [P, KC, 2 * kw])
            qd = Pair(own, tag + "_q", [P, NQ])
            vd = sb(own, tag + "_v", [P, n_st, n_kv, 32])
            qs = sb(own, tag + "_qs", [P, NS, NQ], F32R)
            ks = sb(own, tag + "_ks", [P, n_ks, keys], F32R)
            sel_q, sel_k = Pair(own, tag + "_selq", [P, NS, P]), Pair(own, tag + "_selk", [kw, n_ks, P])
            k_ones = sb(own, tag + "_kones", [P, 1])
            nmx = sb(own, tag + "_nmx", [P, 2, LT, P], F32R)
            pt = sb(own, tag + "_pt", [P, 4, 4, NQ])
            zt = sb(own, tag + "_zt", [P, 4, NQ])
            rz = sb(own, tag + "_rz", [P, NQ])
            a32 = sb(own, tag + "_a32", [P, NQ])
            madd = sb(own, tag + "_mask", [P, LT if row_mask else 1, keys])
            mx = sb(own, tag + "_mx", [P, 2, LT])
            if row_mask:
                mt = Pair(own, tag + "_maskt", [P, n_st, NQ])
            else:
                mcol_i, mcol = sb(own, tag + "_mcoli", [P, ST], I32), sb(own, tag + "_mcol", [P, ST])
            shared = Pair(own, tag + "_k_att", [P, max(groups * NQ, keys)])
            kd = View(shared.h[0:kw, 0:keys], shared.l[0:kw, 0:keys])
            att = View(*(a[:, 0:groups * NQ].rearrange("p (a n) -> p a n", a=groups) for a in (shared.h, shared.l)))
            unused = pt[:, 0:2, :, :].rearrange("p s a n -> p (s a n)")[:, 0:s_slots * keys].rearrange(
                "p (s n) -> p s n", s=s_slots)
            mint = pt[:, 0, 0:2, :].rearrange("p a n -> p (a n)").bitcast(I32)
            brow = pt[:, 0, 2, :]

            plan, n = [], 0
            def ring_step(*x):
                nonlocal n
                plan.append(x + (n,))
                n += 1
                return n - 1
            k_job = [ring_step("k", h) for h in range(n_hf)]
            q_job = ring_step("q")
            ks_job, qs_job, m_job, v_job = {}, {}, {}, []
            def stacks(i):
                if i < n_ks:
                    for h in range(n_hf):
                        ks_job[i, h] = ring_step("ks", i, h)
                qs_job[i] = ring_step("qs", i)
            stacks(0)
            per = heads // NS
            for r, u in enumerate(order):
                i = stack(u)
                if r % per == 0 and i + 1 < NS:
                    stacks(i + 1)
                for lt in range(LT):
                    plan.append(("s", r, u, lt))
                if r % per == 0 and i >= 1:
                    m_job[i - 1] = ring_step("m", i - 1)
                if r < n_st // 4:
                    v_job.append(ring_step("v", r))
            for t_ in range(T + 2):
                if t_ < T:
                    for j in range(4):
                        if t_ == 0 and j == 2:
                            m_job[NS - 1] = ring_step("m", NS - 1)
                        plan.append(("st", t_, j))
                    plan.append(("add", t_))
                if t_ >= 2 and (t_ - 2) % ZG == ZG - 1:
                    plan.append(("z", t_ - 2))
                    if (t_ - 2) % n_st == n_st - 1:
                        plan.append(("oz", (t_ - 2) // n_st))
                if 1 <= t_ <= T:
                    plan.append(("pv", t_ - 1))
            o_job = [ring_step("o", lt) for lt in range(LT)]

            ring = Slots(sem, tag + "_ring", 2, n, mixed=True)
            ring_hi = sem(tag + "_ring_hi")
            score = Slots(sem, tag + "_score", s_slots, heads * LT)
            tile = Slots(sem, tag + "_tile", 4, 4 * T)
            oz_free = sem(tag + "_oz_free")
            max_hi, max_done = sem(tag + "_max_hi"), sem(tag + "_max_done")
            pv_done, added, z_done = sem(tag + "_pv_done"), sem(tag + "_added"), sem(tag + "_z_done")
            rz_done, att_hi, att_done = (sem(tag + x) for x in ("_rz_done", "_att_hi", "_att_done"))
            loaded = {k: sem(f"{tag}_loaded_{k}") for k in ("kqobm" if w_v is None else "kvqobm")}
            split = {k: sem(f"{tag}_split_{k}") for k in "kqvo"}
            sel_done = sem(tag + "_selections_made")
            last_use = {"k": k_job[-1], "q": q_job, "v": v_job[-1], "o": o_job[-1]}
            credits.extend([ring, score, tile])
            extra_credits.extend(list(split.values()) + [z_done, oz_free])
            deep_credits[pv_done.name] = (pv_done, 4)
            deep_credits[added.name] = (added, 16)
            if row_mask:
                turn_m = Slots(sem, tag + "_turn_mask", 2, n_st)
                turn_m_hi = sem(tag + "_turn_mask_hi")
                mask_ready = sem(tag + "_mask_ready")
                credits.append(turn_m)
            n_b = 1 if row_mask else 2
            done = new_barrier()
            bank = lambda m: ps[:, R_BANK + m % 2, :]
            O_BANK, Z_BANK = 4, 5

            def adds_before(t_):
                e = t_ if t_ % ZG else t_ + 1
                return 4 * (e - e // ZG)

            def sp_(sp, b):
                sp.dma_start(brow, bo.unsqueeze(0).broadcast_to([P, D])).then_inc(loaded["b"], 16)
                if row_mask:
                    sp.dma_start(madd[:, :, :], t["mask_Bx1xSxS2_ff0"][b, 0, :, :].rearrange("(r p) s -> p r s", p=P)
                                 ).then_inc(loaded["m"], 16)
                else:
                    m = t["mask_BxS2_ik0"][b, :]
                    sp.dma_start(mint, m.unsqueeze(0).broadcast_to([P, NK])).then_inc(loaded["m"], 16)
                    sp.dma_start(mcol_i[:, :], m.rearrange("(s p) -> p s", p=P),
                                 allow_slow_non_contiguous=True).then_inc(loaded["m"], 16)
                sp.wait_ge(sel_done, b + 1)
                apart(sp)
                with sp.Fori(0, C) as c:
                    g = b * C + c
                    sp.wait_ge(split["k"], g + 1)
                    sp.wait_ge(split["v"], g + 1)
                    if w_v is None:
                        sp.dma_start(raw_kv[:, :, :], w_k.rearrange("(k p) (c n) -> c p k n", p=P, n=2 * kw)[c, :, :, :]
                                     ).then_inc(loaded["k"], 16)
                    else:
                        sp.dma_start(raw_kv[:, :, 0:kw], w_k.rearrange("(k p) (c n) -> c p k n", p=P, n=kw)[c, :, :, :]
                                     ).then_inc(loaded["k"], 16)
                        sp.dma_start(raw_kv[:, :, kw:2 * kw], w_v.rearrange("(k p) (c n) -> c p k n", p=P, n=kw)[c, :, :, :]
                                     ).then_inc(loaded["v"], 16)
                    sp.wait_ge(split["q"], g + 1)
                    sp.dma_start(raw_q[:, :, :], w_q.rearrange("(k p) (c n) -> c p k n", p=P, n=P)[c, :, :, :]
                                 ).then_inc(loaded["q"], 16)
                    sp.wait_ge(split["o"], g + 1)
                    for j in range(4):
                        sp.dma_start(raw_o[32 * j:32 * j + dh, :, :],
                                     w_o.rearrange("(c g j p) n -> c j p g n", c=C, g=groups, j=4)[c, j, :, :, :]
                                     ).then_inc(loaded["o"], 16)
                barrier(sp, done, b)

            def pool_(pool, b):
                for m in (sel_q, sel_k):
                    pool.memset(as_f32(m.h[:, :, :]), 0.0)
                    pool.memset(as_f32(m.l[:, :, :]), 0.0)
                pool.memset(as_f32(nmx[:, :, :, :]), 0.0)
                if two:
                    pool.memset(vd[:, :, :, :], 0.0)
                    pool.memset(raw_o[:, :, :], 0.0)
                pool.tensor_tensor(k_ones[:, :], ident[:, KS:KS + 1], ident[:, KS + 1:KS + 2], ALU.add)
                pool.drain()
                if two:
                    for r in (64 + KS, 65 + KS):
                        pool.tensor_tensor(k_ones[:, :], k_ones[:, :], ident[:, r:r + 1], ALU.add)
                        pool.drain()
                for blk in range(3):
                    for half in range(2 if two else 1):
                        at_ = half * 64 + blk * dh
                        for i in range(NS):
                            dst, j = (sel_q.h if blk in (0, 1) else sel_q.l), i + half * NS
                            pool.tensor_scalar(dst[:, i, at_:at_ + dh], ident[:, j * dh:(j + 1) * dh], float(scale),
                                               None, ALU.mult)
                        for i in range(n_ks):
                            dst, j = (sel_k.h if blk in (0, 2) else sel_k.l), i + half
                            pool.tensor_copy(dst[:, i, at_:at_ + dh], ident[0:kw, j * dh:(j + 1) * dh])
                pool.drain().then_inc(sel_done, 1)
                with pool.Fori(0, C) as c:
                    g = b * C + c
                    if w_v is None:
                        mixed = raw_kv[:, :, :].rearrange("p k (n two) -> p k n two", two=2)
                        src_k, src_v = mixed[:, :, :, 0], mixed[:, :, :, 1]
                    else:
                        src_k, src_v = raw_kv[:, :, 0:kw], raw_kv[:, :, kw:2 * kw]
                    jobs = [("k", "k", wk[:, :, :], src_k), ("q", "q", wq[:, :, :], raw_q[:, :, :]),
                            ("v", "k" if w_v is None else "v", wv[:, :, :], src_v),
                            ("o", "o", wo[:, :, :], raw_o[:, :, :])]
                    for i, (name, load, (hi, lo), src) in enumerate(jobs):
                        dmas = 64 if load == "o" else 16
                        pool.wait_ge(loaded[load], g * dmas + dmas)
                        ring.wait_full_before(pool, g, last_use[name])
                        apart(pool)
                        pool.tensor_copy(hi, src)
                        pool.drain()
                        pool.tensor_tensor(lo, src, as_f32(hi), ALU.subtract).then_inc(split[name], 1)
                barrier(pool, done, b)

            def keys_of(k, h):
                return CT[:, k, h * 512:(h + 1) * 512] if h < 2 else XT[:, k, :]

            def key_tile(k, st):
                return CT[:, k, st * P:(st + 1) * P] if st < ST else XT[:, k, (st - ST) * P:(st - ST + 1) * P]

            def pe_(pe, b):
                if row_mask:
                    pe.wait_ge(mask_ready, b + 1)
                    for st in range(n_st):
                        turn_m.wait_free(pe, b, st)
                        for lt in range(LT):
                            i = pe.transpose(ps[:, T_BANK + st % 2, lt * P:(lt + 1) * P],
                                             madd[:, lt, st * P:(st + 1) * P], ident[:, :])
                        i.then_inc(turn_m.full, 1)
                    turn_m.wait_done(pe, b, n_st - 2, n_st - 1)
                pe.wait_ge(sel_done, b + 1)
                apart(pe)
                with pe.Fori(0, C) as c:
                    g = b * C + c
                    for x in plan:
                        if x[0] == "k":
                            if x[1] == 0:
                                pe.wait_ge(split["k"], g + 2)
                            ring.wait_free(pe, g, x[-1])
                            for k in range(KC):
                                i = mm3(pe, bank(x[-1])[0:kw, :], wk[:, k, :], keys_of(k, x[1]), k == 0, k == KC - 1)
                            i.then_inc(ring.full, 1)
                        elif x[0] == "q":
                            pe.wait_ge(split["q"], g + 2)
                            ring.wait_free(pe, g, x[-1])
                            for k in range(KC):
                                i = mm3(pe, bank(x[-1]), wq[:, k, :], XT[:, k, :], k == 0, k == KC - 1)
                            i.then_inc(ring.full, 1)
                        elif x[0] == "v":
                            if x[1] == 0:
                                pe.wait_ge(split["v"], g + 2)
                            ring.wait_free(pe, g, x[-1])
                            for q in range(4):
                                for k in range(KC):
                                    i = mm3(pe, bank(x[-1])[:, q * kw:(q + 1) * kw], key_tile(k, 4 * x[1] + q),
                                            wv[:, k, :], k == 0 and q == 0, k == KC - 1)
                            i.then_inc(ring.full, 1)
                        elif x[0] == "ks":
                            _, u, h, m = x
                            ring.wait_free(pe, g, m, [k_job[h]] if u == 0 else [])
                            pe.matmul(bank(m), sel_k.h[:, u, :], kd.h[:, h * 512:(h + 1) * 512], start=True,
                                      stop=False, skip_group_check=True)
                            pe.matmul(bank(m), sel_k.l[:, u, :], kd.l[:, h * 512:(h + 1) * 512], start=False,
                                      stop=True, skip_group_check=True).then_inc(ring.full, 1)
                        elif x[0] in ("qs", "m"):
                            _, u, m = x
                            if x[0] == "m":
                                pe.wait_ge(max_done, g * heads + (u + 1) * per)
                            ring.wait_free(pe, g, m, [q_job] if x[0] == "qs" and u == 0 else [])
                            pe.matmul(bank(m), sel_q.h[:, u, :], qd.h[:, :], start=True, stop=False,
                                      skip_group_check=True)
                            i = pe.matmul(bank(m), sel_q.l[:, u, :], qd.l[:, :], start=False, stop=x[0] == "qs",
                                          skip_group_check=True)
                            if x[0] == "m":
                                for lt in range(LT):
                                    i = pe.matmul(bank(m)[:, lt * P:(lt + 1) * P], nmx[:, u % 2, lt, :],
                                                  ident_r[:, :], start=False, stop=True, skip_group_check=True)
                            i.then_inc(ring.full, 1)
                        elif x[0] == "s":
                            _, r, u, lt = x
                            m = r * LT + lt
                            if m == 0:
                                tile.wait_free(pe, g, 3)
                                pe.wait_ge(oz_free, g * groups + 1)
                            if lt == 0:
                                ring.wait_done(pe, g, qs_job[stack(u)],
                                               *(ks_job[min(stack(u), n_ks - 1), h] for h in range(n_hf)))
                            score.wait_free(pe, g, m)
                            p0 = base(u)
                            for h in range(n_hf):
                                i = pe.matmul(ps[:, n_hf * (m % s_slots) + h, :],
                                              qs[p0:p0 + KS, stack(u), lt * P:(lt + 1) * P],
                                              ks[p0:p0 + KS, min(stack(u), n_ks - 1), h * 512:(h + 1) * 512],
                                              start=True, stop=True, skip_group_check=True)
                            i.then_inc(score.full, 1)
                        elif x[0] == "st":
                            _, t_, j = x
                            v, u, m = t_ % n_st, 4 * (t_ // n_st) + j, 4 * t_ + j
                            if t_ == 0:
                                if j == 0:
                                    score.wait_done(pe, g, heads * LT - 1)
                                ring.wait_done(pe, g, m_job[j])
                            tile.wait_free(pe, g, m)
                            if row_mask:
                                pe.matmul(ps[:, j, :], ident_r[:, :], mt.h[:, v, :], start=True, stop=False,
                                          skip_group_check=True)
                                pe.matmul(ps[:, j, :], ident_r[:, :], mt.l[:, v, :], start=False, stop=False,
                                          skip_group_check=True)
                            p0 = base(u)
                            pe.matmul(ps[:, j, :], ks[p0:p0 + KM, min(stack(u), n_ks - 1), v * P:(v + 1) * P],
                                      qs[p0:p0 + KM, stack(u), :], start=not row_mask, stop=True,
                                      skip_group_check=True).then_inc(tile.full, 1)
                        elif x[0] == "pv":
                            t_ = x[1]
                            v, grp = t_ % n_st, t_ // n_st
                            if v == 0:
                                pe.wait_ge(oz_free, g * groups + (grp + 1))
                                if t_ == 0:
                                    ring.wait_done(pe, g, *v_job)
                            for j in range(4):
                                tile.wait_done(pe, g, 4 * t_ + j)
                                i = pe.matmul(ps[32 * j:32 * j + 32, O_BANK, :], vd[:, v, kv_of(4 * grp + j), :],
                                              pt[:, t_ % 4, j, :], start=v == 0, stop=v == n_st - 1,
                                              skip_group_check=True)
                            i.then_inc(pv_done, 1)
                        elif x[0] == "z":
                            t_ = x[1]
                            v, grp = t_ % n_st, t_ // n_st
                            pe.wait_ge(added, g * 3 * T + (16 + adds_before(t_)))
                            if v == ZG - 1:
                                pe.wait_ge(oz_free, g * groups + (grp + 1))
                            for j in range(4):
                                i = pe.matmul(ps[32 * j:32 * j + 32, Z_BANK, :], ones_32[:, :], zt[:, j, :],
                                              start=v == ZG - 1, stop=v == n_st - 1, skip_group_check=True)
                            i.then_inc(z_done, 1)
                        elif x[0] == "o":
                            _, lt, m = x
                            if lt == 0:
                                pe.wait_ge(split["o"], g + 2)
                                pe.wait_ge(att_done, g * groups + groups)
                            ring.wait_free(pe, g, m)
                            for grp in range(groups):
                                i = mm3(pe, bank(m), att[:, grp, lt * P:(lt + 1) * P], wo[:, grp, :], grp == 0,
                                        grp == groups - 1)
                            i.then_inc(ring.full, 1)
                barrier(pe, done, b)

            def act_(act, b):
                if row_mask:
                    for st in range(n_st):
                        turn_m.wait_full(act, b, st)
                        act.activation(mt.h[:, st, :], ps[:, T_BANK + st % 2, :], ACT.Copy).then_inc(turn_m_hi, 1)
                with act.Fori(0, C) as c:
                    g = b * C + c
                    for x in plan:
                        if x[0] == "k":
                            ring.wait_full(act, g, x[-1])
                            apart(act)
                            act.activation(kd.h[:, x[1] * 512:(x[1] + 1) * 512], bank(x[-1])[0:kw, :], ACT.Identity,
                                           bias=cols[0:kw, bass.ds(c + c_bk, 1)]).then_inc(ring_hi, 1)
                        elif x[0] == "q":
                            ring.wait_full(act, g, x[-1])
                            apart(act)
                            act.activation(qd.h[:, :], bank(x[-1]), ACT.Identity,
                                           bias=cols[:, bass.ds(c + c_bq, 1)]).then_inc(ring_hi, 1)
                        elif x[0] == "ks":
                            _, u, h, m = x
                            ring.wait_full(act, g, m)
                            act.activation(ks[:, u, h * 512:(h + 1) * 512], bank(m), ACT.Identity,
                                           bias=k_ones[:, :]).then_inc(ring.freed(m), 1)
                        elif x[0] in ("qs", "m"):
                            ring.wait_full(act, g, x[-1])
                            act.activation(qs[:, x[1], :], bank(x[-1]), ACT.Copy).then_inc(ring.freed(x[-1]), 1)
                        elif x[0] == "st":
                            _, t_, j = x
                            m = 4 * t_ + j
                            if j == 0:
                                act.wait_ge(pv_done, g * T + (t_ + 1))
                                act.wait_ge(added, g * 3 * T + (16 + adds_before(t_ - 4)))
                            tile.wait_full(act, g, m)
                            v = t_ % n_st
                            bias = mcol[:, v:v + 1] if not row_mask and v < ST else zero_col[:, :]
                            act.activation(pt[:, t_ % 4, j, :], ps[:, j, :], ACT.Exp, bias=bias,
                                           scale=1.0).then_inc(tile.freed(m), 1)
                        elif x[0] == "oz":
                            grp = x[1]
                            act.wait_ge(oz_free, g * groups + (grp + 2))
                            ring.wait_full_before(act, g, o_job[-1])
                            apart(act)
                            act.activation(att.h[:, grp, :], a32[:, :], ACT.Identity,
                                           bias=cols[:, bass.ds(c * groups + (c_bv + grp), 1)]).then_inc(att_hi, 1)
                barrier(act, done, b)

            def dve_(dve, b):
                dve.wait_ge(loaded["m"], b * (16 * n_b) + 16 * n_b)
                apart(dve)
                if row_mask:
                    for lt in range(LT):
                        i = dve.tensor_scalar(madd[:, lt, :], madd[:, lt, :], -1.0e38, None, ALU.max)
                    i.then_inc(mask_ready, 1)
                    for st in range(n_st):
                        dve.wait_ge(turn_m_hi, b * n_st + st + 1)
                        dve.tensor_tensor(mt.l[:, st, :], ps[:, T_BANK + st % 2, :], as_f32(mt.h[:, st, :]),
                                          ALU.subtract).then_inc(turn_m.freed(st), 1)
                else:
                    dve.tensor_scalar(madd[:, 0, 0:NK], mint, 0.0, BLOCKED, ALU.is_equal, ALU.mult)
                    dve.tensor_scalar(mcol[:, :], mcol_i[:, :], 0.0, BLOCKED, ALU.is_equal, ALU.mult)
                    dve.memset(madd[:, 0, NK:keys], 0.0)
                dve.wait_ge(loaded["b"], b * 16 + 16)
                for lt in range(LT):
                    dve.tensor_tensor(acc[:, lt, :], X[:, lt, :], brow, ALU.add)
                dve.drain()
                with dve.Fori(0, C) as c:
                    g = b * C + c
                    n_hi = 0
                    for x in plan:
                        if x[0] == "k":
                            n_hi += 1
                            dve.wait_ge(ring_hi, g * (n_hf + 1) + n_hi)
                            sl = slice(x[1] * 512, (x[1] + 1) * 512)
                            dve.scalar_tensor_tensor(out=kd.l[:, sl], in0=bank(x[-1])[0:kw, :],
                                                     scalar=cols[0:kw, bass.ds(c + c_bk, 1)],
                                                     in1=as_f32(kd.h[:, sl]), op0=ALU.add,
                                                     op1=ALU.subtract).then_inc(ring.freed(x[-1]), 1)
                        elif x[0] == "q":
                            n_hi += 1
                            dve.wait_ge(ring_hi, g * (n_hf + 1) + n_hi)
                            dve.scalar_tensor_tensor(out=qd.l[:, :], in0=bank(x[-1]),
                                                     scalar=cols[:, bass.ds(c + c_bq, 1)],
                                                     in1=as_f32(qd.h[:, :]), op0=ALU.add,
                                                     op1=ALU.subtract).then_inc(ring.freed(x[-1]), 1)
                        elif x[0] == "v":
                            ring.wait_full(dve, g, x[-1])
                            dve.tensor_copy(vd[:, 4 * x[1]:4 * x[1] + 4, :, 0:dh],
                                            bank(x[-1])[:, 0:4 * kw].rearrange("p (q w d) -> p q w d", q=4, d=dh)
                                            ).then_inc(ring.freed(x[-1]), 1)
                        elif x[0] == "s":
                            _, r, u, lt = x
                            m = r * LT + lt
                            score.wait_full(dve, g, m)
                            s0_ = n_hf * (m % s_slots)
                            apart(dve)
                            dve.tensor_tensor_reduce(
                                unused[:, m % s_slots, :].rearrange("p (h w) -> p h w", h=n_hf), ps[:, s0_:s0_ + n_hf, :],
                                madd[:, lt if row_mask else 0, :].rearrange("p (h w) -> p h w", h=n_hf),
                                1.0, BLOCKED, ALU.add, ALU.max, mx[:, r % 2, lt:lt + 1]).then_inc(score.freed(m), 1)
                            if lt == LT - 1:
                                col = base(u) + KS
                                i = stack(u)
                                if i >= 2:
                                    ring.wait_full(dve, g, m_job[i - 2])
                                else:
                                    ring.wait_full_before(dve, g, m_job[i + 2])
                                score.wait_done(dve, g, m)
                                dve.tensor_scalar(nmx[:, i % 2, :, col], mx[:, r % 2, :], -1.0, None,
                                                  ALU.mult).then_inc(max_hi, 1)
                                dve.wait_ge(max_hi, g * heads + r + 1)
                                dve.scalar_tensor_tensor(out=nmx[:, i % 2, :, col + 1], in0=mx[:, r % 2, :], scalar=-1.0,
                                                         in1=as_f32(nmx[:, i % 2, :, col]), op0=ALU.mult,
                                                         op1=ALU.subtract).then_inc(max_done, 1)
                        elif x[0] == "add" and x[1] % ZG:
                            t_ = x[1]
                            for j in range(4):
                                tile.wait_done(dve, g, 4 * t_ + j)
                                if t_ % ZG == 1:
                                    if j == 0:
                                        dve.wait_ge(z_done, g * (T // ZG) + (t_ // ZG + 1))
                                    first = pt[:, (t_ - 1) % 4, j, :]
                                else:
                                    dve.wait_ge(added, g * 3 * T + (16 + adds_before(t_) - 7 + j))
                                    first = zt[:, j, :]
                                dve.tensor_tensor(zt[:, j, :], first, pt[:, t_ % 4, j, :], ALU.add).then_inc(added, 1)
                        elif x[0] == "oz":
                            grp = x[1]
                            dve.wait_ge(z_done, g * (T // ZG) + ((grp + 1) * (n_st // ZG) + 1))
                            dve.reciprocal(rz[:, :], ps[:, Z_BANK, :]).then_inc(rz_done, 1)
                            dve.wait_ge(rz_done, g * groups + grp + 1)
                            dve.tensor_tensor(a32[:, :], ps[:, O_BANK, :], rz[:, :], ALU.mult).then_inc(oz_free, 1)
                            dve.wait_ge(att_hi, g * groups + grp + 1)
                            dve.scalar_tensor_tensor(out=att.l[:, grp, :], in0=a32[:, :],
                                                     scalar=cols[:, bass.ds(c * groups + (c_bv + grp), 1)],
                                                     in1=as_f32(att.h[:, grp, :]), op0=ALU.add,
                                                     op1=ALU.subtract).then_inc(att_done, 1)
                        elif x[0] == "o":
                            _, lt, m = x
                            ring.wait_full(dve, g, m)
                            dve.tensor_tensor(acc[:, lt, :], bank(m), acc[:, lt, :], ALU.add).then_inc(ring.freed(m), 1)
                    dve.drain()
                barrier(dve, done, b)

            add(sp_, pool_, pe_, act_, dve_)
            own.close()

        def wide(i_):
            tag, nth = "w", int(i_) - 1
            own = ExitStack()
            H, C = 16, 8
            SC = float(1.0 / np.sqrt(np.float32(P)))
            W = {"k": t["L2_xattn_wk" + i_], "q": t["L2_xattn_wq" + i_], "v": t["L2_xattn_wv" + i_],
                 "o": t["L2_xattn_wo" + i_]}
            c_bq, c_bk, c_xk, c_xv = (at[n + "_2" + i_] for n in ("bq", "bk", "xk", "xv"))
            raw = sb(own, tag + "_raw", [P, 2, 1024])
            w = {k: Pair(own, f"{tag}_w{k}", [P, KC, 256] if k != "o" else [P, 2, D]) for k in "kqvo"}
            kt, qt = Pair(own, tag + "_k", [P, 2, NK]), Pair(own, tag + "_q", [P, 2, NQ])
            vv = Pair(own, tag + "_v", [P, ST, 256])
            v32 = sb(own, tag + "_v32", [P, 2, 2, 256])
            prob = sb(own, tag + "_p", [P, 2, LT, NK])
            pt = Pair(own, tag + "_pt", [P, 4, NQ])
            att = Pair(own, tag + "_att", [P, NQ])
            vrow = sb(own, tag + "_vrow", [P, 2, 256])
            cv = sb(own, tag + "_cv", [P, 256])
            xk = Pair(own, tag + "_xk", [P, H, 2])
            xv = Pair(own, tag + "_xv", [P, 2])
            xl = sb(own, tag + "_xl", [P, 2, LT])
            crow = sb(own, tag + "_crow", [1, D])
            crow_p = Pair(own, tag + "_crowp", [1, D])
            mx, nm, z, ex, zx, rz = (sb(own, tag + n, [P, 2, LT]) for n in ("_mx", "_nm", "_z", "_ex", "_zx", "_rz"))

            plan, n = [], 0
            job = {}
            def ring_step(*x):
                nonlocal n
                job[x] = n
                plan.append(x)
                n += 1
            for x in (("k", 0, 0), ("k", 0, 1), ("q", 0), ("x", 0)):
                ring_step(*x)
            plan += [("s", 0, 0), ("s", 0, 1)]
            ring_step("k", 1, 0)
            plan.append(("s", 0, 2))
            ring_step("k", 1, 1)
            plan.append(("s", 0, 3))
            ring_step("q", 1)
            ring_step("x", 1)
            for v in range(4):
                ring_step("v", v)
            for u in range(2):
                def pv(v):
                    if v == 0:
                        nonlocal n
                        job["pv", u] = n
                        n += 1
                    plan.append(("pv", u, v))
                if u == 1:
                    plan += [("t", 1, 0), ("t", 1, 1)]
                    ring_step("c")
                    for lt in range(LT):
                        ring_step("o", 0, lt)
                for v in range(ST):
                    if u == 0 or v >= 2:
                        plan.append(("t", u, v))
                    if u == 0 and v % 2 == 1:
                        plan.append(("s", 1, v // 2))
                    if v >= 2:
                        pv(v - 2)
                pv(ST - 2)
                pv(ST - 1)
            for lt in range(LT):
                ring_step("o", 1, lt)

            ring = Slots(sem, tag + "_ring", 2, n)
            ring_hi = sem(tag + "_ring_hi")
            turn = Slots(sem, tag + "_turn", 2, 2 * ST)
            turn_hi = sem(tag + "_turn_hi")
            score = Slots(sem, tag + "_score", 2, 2 * LT)
            max_own, max_done = sem(tag + "_max_own"), sem(tag + "_max_done")
            v_hi, v_done = sem(tag + "_v_hi"), sem(tag + "_v_done")
            own_d = sem(tag + "_dve_own")
            loaded = {k: sem(f"{tag}_loaded_{k}") for k in "kqvo"}
            rows_loaded, crow_loaded = sem(tag + "_rows_loaded"), sem(tag + "_crow_loaded")
            cv_done, xv_done, xk_done = (sem(tag + x) for x in ("_cv_done", "_xv_done", "_xk_done"))
            split = {k: sem(f"{tag}_split_{k}") for k in "kqvo"}
            row_done, row_full = sem(tag + "_row_done"), sem(tag + "_row_full")
            last_use = {"k": job["k", 1, 1], "q": job["q", 1], "v": job["v", 3], "o": job["o", 1, 3]}
            credits.extend([ring, turn, score])
            extra_credits.extend(list(split.values()) + [cv_done])
            done = new_barrier()
            bank = lambda m: ps[:, R_BANK + m % 2, :]

            def view(name):
                if name == "o":
                    return W["o"].rearrange("(c k p) n -> c p k n", p=P, k=2)
                return W[name].rearrange("(k p) (c n) -> c p k n", p=P, n=256)

            def raw_of(i, name):
                return raw[:, i % 2, :].rearrange("p (k n) -> p k n", k=2 if name == "o" else KC)

            def sp_(sp, b):
                bb = b * 2 + nth
                sp.dma_start(crow[:, :], t["L2_xattn_bo" + i_].unsqueeze(0)).then_inc(crow_loaded, 16)
                with sp.Fori(0, C) as c:
                    g = bb * C + c
                    for i, name in enumerate("kqvo"):
                        sp.wait_ge(split["vokq"[i]], g + (1 if i < 2 else 2))
                        sp.dma_start(raw_of(i, name), view(name)[c, :, :, :]).then_inc(loaded[name], 16)
                        if i == 1:
                            sp.wait_ge(cv_done, g + 1)
                            for r, src in enumerate((t["L2_xattn_bv" + i_].rearrange("(c n) -> c n", n=256),
                                                     t["L2_xattn_bias_v" + i_].rearrange("a b (c h) k -> (a b c) (h k)", h=2))):
                                sp.dma_start(vrow[:, r, :], src[c, :].unsqueeze(0).broadcast_to([P, 256])
                                             ).then_inc(rows_loaded, 16)
                barrier(sp, done, b)

            def pool_(pool, b):
                bb = b * 2 + nth
                with pool.Fori(0, C) as c:
                    g = bb * C + c
                    for i, name in enumerate("kqvo"):
                        pool.wait_ge(loaded[name], g * 16 + 16)
                        ring.wait_full_before(pool, g, last_use[name])
                        hi, lo = w[name][:, :, :]
                        apart(pool)
                        pool.tensor_copy(hi, raw_of(i, name))
                        pool.drain()
                        pool.tensor_tensor(lo, raw_of(i, name), as_f32(hi), ALU.subtract).then_inc(split[name], 1)
                barrier(pool, done, b)

            def pe_(pe, b):
                bb = b * 2 + nth
                pe.wait_ge(xk_done, bb + 1)
                apart(pe)
                with pe.Fori(0, C) as c:
                    g = bb * C + c
                    for x in plan:
                        m = job.get(x)
                        if x[0] in "kq" and x[-1] == 0 and x[1] == 0:
                            pe.wait_ge(split[x[0]], g + 2)
                        if x[0] == "k":
                            _, u, h = x
                            ring.wait_free(pe, g, m)
                            for k in range(KC):
                                i = mm3(pe, bank(m), w["k"][:, k, u * P:(u + 1) * P], CT[:, k, h * 512:(h + 1) * 512],
                                        k == 0, k == KC - 1)
                            i.then_inc(ring.full, 1)
                        elif x[0] == "q":
                            ring.wait_free(pe, g, m)
                            for k in range(KC):
                                i = mm3(pe, bank(m), w["q"][:, k, x[1] * P:(x[1] + 1) * P], XT[:, k, :],
                                        k == 0, k == KC - 1)
                            i.then_inc(ring.full, 1)
                        elif x[0] == "x":
                            u = x[1]
                            ring.wait_free(pe, g, m, [job["q", u]])
                            for lt in range(LT):
                                i = mm3(pe, bank(m)[:, 2 * lt:2 * lt + 2], qt[:, u, lt * P:(lt + 1) * P],
                                        (xk.h[:, bass.ds(c * 2 + u, 1), :], xk.l[:, bass.ds(c * 2 + u, 1), :]),
                                        lt == 0, True)
                            i.then_inc(ring.full, 1)
                        elif x[0] == "v":
                            if x[1] == 0:
                                pe.wait_ge(split["v"], g + 2)
                            ring.wait_free(pe, g, m)
                            for q in range(2):
                                for k in range(KC):
                                    i = mm3(pe, bank(m)[:, q * 256:(q + 1) * 256],
                                            CT[:, k, (2 * x[1] + q) * P:(2 * x[1] + q + 1) * P], w["v"][:, k, :],
                                            k == 0 and q == 0, k == KC - 1)
                            i.then_inc(ring.full, 1)
                        elif x[0] == "s":
                            _, u, lt = x
                            if lt == 0:
                                ring.wait_done(pe, g, job["k", u, 0], job["k", u, 1])
                            sn = u * LT + lt
                            score.wait_free(pe, g, sn)
                            for h in range(2):
                                i = mm3(pe, ps[:, S_BANK + 2 * (sn % 2) + h, :], qt[:, u, lt * P:(lt + 1) * P],
                                        kt[:, u, h * 512:(h + 1) * 512], True, True)
                            i.then_inc(score.full, 1)
                        elif x[0] == "t":
                            _, u, v = x
                            tn = u * ST + v
                            if v == 0:
                                score.wait_done(pe, g, u * LT + 2, u * LT + 3)
                            turn.wait_free(pe, g, tn)
                            for lt in range(LT):
                                i = pe.transpose(ps[:, T_BANK + tn % 2, lt * P:(lt + 1) * P],
                                                 prob[:, u, lt, v * P:(v + 1) * P], ident[:, :])
                            i.then_inc(turn.full, 1)
                        elif x[0] == "pv":
                            _, u, v = x
                            tn, m = u * ST + v, job["pv", u]
                            if v == 0:
                                ring.wait_free(pe, g, m)
                                pe.wait_ge(v_done, g * 4 + 4)
                            turn.wait_done(pe, g, tn)
                            i = mm3(pe, bank(m), vv[:, v, u * P:(u + 1) * P], pt[:, tn % 4, :], v == 0, v == ST - 1)
                            if v == ST - 1:
                                i.then_inc(ring.full, 1)
                        elif x[0] == "c":
                            pe.wait_ge(split["o"], g + 2)
                            pe.wait_ge(xv_done, g + 1)
                            ring.wait_free(pe, g, m)
                            for h in range(2):
                                i = mm3(pe, bank(m)[0:1, :], xv[:, h:h + 1], w["o"][:, h, :], h == 0, h == 1)
                            i.then_inc(ring.full, 1)
                        else:
                            _, u, lt = x
                            ring.wait_free(pe, g, m, [job["pv", u]] if lt == 0 else [])
                            mm3(pe, bank(m), att[:, lt * P:(lt + 1) * P], w["o"][:, u, :], True,
                                True).then_inc(ring.full, 1)
                pe.wait_ge(row_done, bb + 1)
                pe.matmul(ps[:, S_BANK, :], ones_row[:, :], crow_p.h[:, :], start=True, stop=False)
                pe.matmul(ps[:, S_BANK, :], ones_row[:, :], crow_p.l[:, :], start=False, stop=True).then_inc(row_full, 1)
                barrier(pe, done, b)

            def act_(act, b):
                bb = b * 2 + nth
                with act.Fori(0, C) as c:
                    g = bb * C + c
                    for x in plan:
                        m = job.get(x)
                        if x[0] == "k":
                            _, u, h = x
                            ring.wait_full(act, g, m)
                            apart(act)
                            act.activation(kt.h[:, u, h * 512:(h + 1) * 512], bank(m), ACT.Identity,
                                           bias=cols[:, bass.ds(c * 2 + (c_bk + u), 1)]).then_inc(ring_hi, 1)
                        elif x[0] == "q":
                            ring.wait_full(act, g, m)
                            apart(act)
                            act.activation(qt.h[:, x[1], :], bank(m), ACT.Identity,
                                           bias=cols[:, bass.ds(c * 2 + (c_bq + x[1]), 1)]).then_inc(ring_hi, 1)
                        elif x[0] == "v":
                            ring.wait_done(act, g, m)
                            act.activation(vv.h[:, 2 * x[1]:2 * x[1] + 2, :], v32[:, x[1] % 2, :, :],
                                           ACT.Copy).then_inc(v_hi, 1)
                        elif x[0] == "s":
                            _, u, lt = x
                            sn = u * LT + lt
                            act.wait_ge(max_done, g * 2 * LT + sn + 1)
                            act.activation(ex[:, u, lt:lt + 1], xl[:, u, lt:lt + 1], ACT.Exp,
                                           bias=nm[:, u, lt:lt + 1], scale=SC)
                            act.activation(prob[:, u, lt, :].rearrange("p (h w) -> p h w", h=2),
                                           ps[:, S_BANK + 2 * (sn % 2):S_BANK + 2 * (sn % 2) + 2, :], ACT.Exp,
                                           bias=nm[:, u, lt:lt + 1], scale=SC,
                                           accum_out=z[:, u, lt:lt + 1]).then_inc(score.freed(sn), 1)
                        elif x[0] == "t":
                            tn = x[1] * ST + x[2]
                            turn.wait_full(act, g, tn)
                            act.activation(pt.h[:, tn % 4, :], ps[:, T_BANK + tn % 2, :], ACT.Copy).then_inc(turn_hi, 1)
                        elif x[0] == "pv" and x[2] == ST - 1:
                            ring.wait_full(act, g, job["pv", x[1]])
                            act.activation(att.h[:, :], bank(job["pv", x[1]]), ACT.Copy).then_inc(ring_hi, 1)
                barrier(act, done, b)

            def dve_(dve, b):
                bb = b * 2 + nth
                src = cols[:, c_xk:c_xk + H].unsqueeze(2).broadcast_to([P, H, 2])
                dve.tensor_copy(xk.h[:, :, :], src)
                dve.drain()
                dve.tensor_tensor(xk.l[:, :, :], src, as_f32(xk.h[:, :, :]), ALU.subtract).then_inc(xk_done, 1)
                dve.wait_ge(crow_loaded, bb * 16 + 16)
                apart(dve)
                with dve.Fori(0, C) as c:
                    g = bb * C + c
                    pair_xv = cols[:, bass.ds(c * 2 + c_xv, 2)]
                    dve.wait_ge(rows_loaded, g * 32 + 32)
                    dve.tensor_tensor(cv[:, :], vrow[:, 0, :], vrow[:, 1, :], ALU.subtract).then_inc(cv_done, 1)
                    dve.tensor_copy(xv.h[:, :], pair_xv)
                    dve.drain()
                    dve.tensor_tensor(xv.l[:, :], pair_xv, as_f32(xv.h[:, :]), ALU.subtract).then_inc(xv_done, 1)
                    n_hi = 0
                    for x in plan:
                        m = job.get(x)
                        if x[0] == "k":
                            _, u, h = x
                            n_hi += 1
                            dve.wait_ge(ring_hi, g * 8 + n_hi)
                            sl = slice(h * 512, (h + 1) * 512)
                            dve.scalar_tensor_tensor(out=kt.l[:, u, sl], in0=bank(m),
                                                     scalar=cols[:, bass.ds(c * 2 + (c_bk + u), 1)],
                                                     in1=as_f32(kt.h[:, u, sl]), op0=ALU.add,
                                                     op1=ALU.subtract).then_inc(ring.freed(m), 1)
                        elif x[0] == "q":
                            n_hi += 1
                            dve.wait_ge(ring_hi, g * 8 + n_hi)
                            dve.scalar_tensor_tensor(out=qt.l[:, x[1], :], in0=bank(m),
                                                     scalar=cols[:, bass.ds(c * 2 + (c_bq + x[1]), 1)],
                                                     in1=as_f32(qt.h[:, x[1], :]), op0=ALU.add,
                                                     op1=ALU.subtract).then_inc(ring.freed(m), 1)
                        elif x[0] == "x":
                            ring.wait_full(dve, g, m)
                            dve.tensor_copy(xl[:, x[1], :], bank(m)[:, 0:2 * LT].rearrange("p (l e) -> p l e", e=2)[:, :, 0]
                                            ).then_inc(ring.freed(m), 1)
                        elif x[0] == "v":
                            ring.wait_full(dve, g, m)
                            dve.tensor_tensor(v32[:, x[1] % 2, :, :], bank(m).rearrange("p (q w) -> p q w", q=2),
                                              cv[:, :].unsqueeze(1).broadcast_to([P, 2, 256]),
                                              ALU.add).then_inc(ring.freed(m), 1)
                            dve.wait_ge(v_hi, g * 4 + x[1] + 1)
                            dve.tensor_tensor(vv.l[:, 2 * x[1]:2 * x[1] + 2, :], v32[:, x[1] % 2, :, :],
                                              as_f32(vv.h[:, 2 * x[1]:2 * x[1] + 2, :]), ALU.subtract).then_inc(v_done, 1)
                        elif x[0] == "s":
                            _, u, lt = x
                            sn = u * LT + lt
                            score.wait_full(dve, g, sn)
                            dve.tensor_reduce(mx[:, u, lt:lt + 1],
                                              ps[:, S_BANK + 2 * (sn % 2):S_BANK + 2 * (sn % 2) + 2, :], AX.XY,
                                              ALU.max).then_inc(max_own, 1)
                            if lt == 0:
                                ring.wait_done(dve, g, job["x", u])
                            dve.wait_ge(max_own, g * 2 * LT + sn + 1)
                            dve.tensor_scalar(nm[:, u, lt:lt + 1], mx[:, u, lt:lt + 1], xl[:, u, lt:lt + 1], -SC,
                                              ALU.max, ALU.mult).then_inc(max_done, 1)
                        elif x[0] == "t":
                            tn = x[1] * ST + x[2]
                            dve.wait_ge(turn_hi, g * 2 * ST + tn + 1)
                            dve.tensor_tensor(pt.l[:, tn % 4, :], ps[:, T_BANK + tn % 2, :], as_f32(pt.h[:, tn % 4, :]),
                                              ALU.subtract).then_inc(turn.freed(tn), 1)
                        elif x[0] == "pv" and x[2] == ST - 1:
                            u = x[1]
                            score.wait_done(dve, g, u * LT + 3)
                            dve.tensor_tensor(zx[:, u, :], z[:, u, :], ex[:, u, :], ALU.add).then_inc(own_d, 1)
                            dve.wait_ge(own_d, g * 4 + 2 * u + 1)
                            dve.reciprocal(rz[:, u, :], zx[:, u, :]).then_inc(own_d, 1)
                            n_hi += 1
                            dve.wait_ge(ring_hi, g * 8 + n_hi)
                            dve.tensor_tensor(att.l[:, :], bank(job["pv", u]), as_f32(att.h[:, :]),
                                              ALU.subtract).then_inc(ring.freed(job["pv", u]), 1)
                            dve.wait_ge(own_d, g * 4 + 2 * u + 2)
                        elif x[0] == "c":
                            ring.wait_full(dve, g, m)
                            dve.tensor_tensor(crow[:, :], bank(m)[0:1, :], crow[:, :], ALU.add).then_inc(ring.freed(m), 1)
                        elif x[0] == "o":
                            _, u, lt = x
                            ring.wait_full(dve, g, m)
                            if u == 1:
                                ring.wait_done(dve, g, job["o", 0, lt])
                            dve.scalar_tensor_tensor(out=X[:, lt, :], in0=bank(m), scalar=rz[:, u, lt:lt + 1],
                                                     in1=X[:, lt, :], op0=ALU.mult,
                                                     op1=ALU.add).then_inc(ring.freed(m), 1)
                    dve.drain()
                dve.tensor_copy(crow_p.h[:, :], crow[:, :])
                dve.drain()
                dve.tensor_tensor(crow_p.l[:, :], crow[:, :], as_f32(crow_p.h[:, :]), ALU.subtract).then_inc(row_done, 1)
                dve.wait_ge(row_full, bb + 1)
                for lt in range(LT):
                    dve.tensor_tensor(X[:, lt, :], ps[:, S_BANK, :], X[:, lt, :], ALU.add)
                barrier(dve, done, b)

            add(sp_, pool_, pe_, act_, dve_)
            own.close()

        norms = [0, 0]

        def norm(tag, src, eps, c_scale, c_shift, rms=False, first=None):
            own = ExitStack()
            xn = sb(own, tag + "_xn", [P, LT, D])
            tmp = sb(own, tag + "_tmp", [P, 2, NQ])
            stats, mv = sb(own, tag + "_st", [P, LT, 6]), sb(own, tag + "_mv", [P, LT, 2])
            ve, sd, rs = (sb(own, tag + n, [P, LT]) for n in ("_ve", "_sd", "_rs"))
            gb = sb(own, tag + "_gb", [P, 2, D]) if first else None
            turn_n = Turn(xn, XT, scale=c_scale, shift=c_shift, tmp=tmp)
            rows_ld = sem(tag + "_rows_loaded") if first else None
            var_done, sqrt_done, xn_done = (sem(n) for n in ("var_done", "sqrt_done", "xn_done"))
            rounds = 2 if first else 1
            nth, round0 = norms[0], norms[1]
            norms[0] += 1
            norms[1] += rounds
            done = new_barrier()

            def sp_(sp, b):
                if first:
                    for i in range(2):
                        sp.dma_start(gb[:, i, :], first[i].unsqueeze(0).broadcast_to([P, D])).then_inc(rows_ld, 16)
                barrier(sp, done, b)

            def pool_(pool, b):
                barrier(pool, done, b)

            def pe_(pe, b):
                pe.wait_ge(xn_done, b * norms[0] + (nth + 1))
                turn_n.pe(pe, b)
                barrier(pe, done, b)

            def act_(act, b):
                for r in range(rounds):
                    act.wait_ge(var_done, b * norms[1] + (round0 + r + 1))
                    act.activation(sd[:, :], ve[:, :], ACT.Sqrt).then_inc(sqrt_done, 1)
                turn_n.act(act, b)
                barrier(act, done, b)

            def dve_(dve, b):
                for r in range(rounds):
                    e = first[2] if first and r == 0 else eps
                    if rms:
                        for lt in range(LT):
                            dve.tensor_tensor_reduce(xn[:, lt, :], src[:, lt, :], src[:, lt, :], 1.0, 0.0, ALU.mult,
                                                     ALU.add, ve[:, lt:lt + 1])
                        dve.drain()
                        dve.tensor_scalar(ve[:, :], ve[:, :], 1.0 / D, float(e), ALU.mult, ALU.add).then_inc(var_done, 1)
                    else:
                        for lt in range(LT):
                            dve.bn_stats(stats[:, lt, :], src[:, lt, :])
                        dve.drain()
                        for lt in range(LT):
                            dve.bn_aggr(mv[:, lt, :], stats[:, lt, :])
                        dve.drain()
                        dve.tensor_scalar(ve[:, :], mv[:, :, 1], float(e), None, ALU.add).then_inc(var_done, 1)
                    dve.wait_ge(sqrt_done, b * norms[1] + (round0 + r + 1))
                    dve.reciprocal(rs[:, :], sd[:, :])
                    dve.drain()
                    for lt in range(LT):
                        if rms:
                            dve.tensor_scalar(xn[:, lt, :], src[:, lt, :], rs[:, lt:lt + 1], None, ALU.mult)
                        else:
                            dve.tensor_scalar(xn[:, lt, :], src[:, lt, :], mv[:, lt, 0:1], rs[:, lt:lt + 1],
                                              ALU.subtract, ALU.mult)
                    if r < rounds - 1:
                        dve.drain()
                        dve.wait_ge(rows_ld, b * 32 + 32)
                        for lt in range(LT):
                            dve.tensor_tensor(xn[:, lt, :], xn[:, lt, :], gb[:, 0, :], ALU.mult)
                        dve.drain()
                        for lt in range(LT):
                            dve.tensor_tensor(src[:, lt, :], xn[:, lt, :], gb[:, 1, :], ALU.add)
                        dve.drain()
                dve.drain().then_inc(xn_done, 1)
                turn_n.dve(dve, b)
                barrier(dve, done, b)

            add(sp_, pool_, pe_, act_, dve_)
            own.close()

        def mlp(nth, func, w1, w2, c_b1, b2, last):
            tag = "mlp"
            own = ExitStack()
            C = F // P // 2
            raw1, raw2 = sb(own, tag + "_raw1", [P, 2, KC, P]), sb(own, tag + "_raw2", [P, 2, D])
            p1 = [Pair(own, f"{tag}_w1{i}", [P, KC, P]) for i in range(2)]
            p2 = [Pair(own, f"{tag}_w2{i}", [P, D]) for i in range(2)]
            g32 = sb(own, tag + "_g32", [P, 2, NQ])
            gp = Pair(own, tag + "_g", [P, 2, NQ])
            brow, browp = sb(own, tag + "_b2", [1, D]), Pair(own, tag + "_b2p", [1, D])
            res = sb(own, tag + "_res", [P, LT, D]) if last else X
            ring = Slots(sem, tag + "_ring", 2, 2)
            ld1, ld2 = ([sem(f"{tag}_w{w}_loaded{i}") for i in range(2)] for w in "12")
            sp1, sp2 = ([sem(f"{tag}_w{w}_split{i}") for i in range(2)] for w in "12")
            w2_hi, g_hi = sem(tag + "_w2_hi"), sem(tag + "_g_hi")
            hid_done, prod_done = sem(tag + "_hidden_done"), sem(tag + "_product_done")
            b_ld, b_done, sum_done, stored = (sem(tag + n) for n in ("_b2_loaded", "_b2_done", "_sum_done", "_stored"))
            credits.append(ring)
            extra_credits.extend(sp1 + sp2)
            deep_credits[prod_done.name] = (prod_done, 2)
            done = new_barrier()

            def sp_(sp, b):
                bb = b * 2 + nth
                sp.dma_start(brow[:, :], b2.unsqueeze(0)).then_inc(b_ld, 16)
                with sp.Fori(0, C) as c:
                    g = bb * C + c
                    for i in range(2):
                        sp.wait_ge(sp1[i], g + 1)
                        sp.dma_start(raw1[:, i, :, :], w1.rearrange("(k p) (c n) -> c p k n", p=P, n=P)[c * 2 + i, :, :, :]
                                     ).then_inc(ld1[i], 16)
                        sp.wait_ge(sp2[i], g + 1)
                        sp.dma_start(raw2[:, i, :], w2.rearrange("(c p) n -> c p n", p=P)[c * 2 + i, :, :]
                                     ).then_inc(ld2[i], 16)
                if last:
                    sp.wait_ge(sum_done, bb + 1)
                    sp.dma_start(out[b, :, :].rearrange("(r p) d -> p r d", p=P), res[:, :, :]).then_inc(stored, 16)
                    sp.wait_ge(stored, b * 16 + 16)
                barrier(sp, done, b)

            def pool_(pool, b):
                bb = b * 2 + nth
                with pool.Fori(0, C) as c:
                    g = bb * C + c
                    for i in range(2):
                        pool.wait_ge(ld1[i], g * 16 + 16)
                        ring.wait_full_before(pool, g, i)
                        apart(pool)
                        pool.tensor_copy(p1[i].h[:, :, :], raw1[:, i, :, :])
                        pool.drain()
                        pool.tensor_tensor(p1[i].l[:, :, :], raw1[:, i, :, :], as_f32(p1[i].h[:, :, :]),
                                           ALU.subtract).then_inc(sp1[i], 1)
                barrier(pool, done, b)

            def pe_(pe, b):
                bb = b * 2 + nth
                pe.wait_ge(b_done, bb + 1)
                for lt in range(LT):
                    pe.matmul(ps[:, lt, :], ones_row[:, :], browp.h[:, :], start=True, stop=False, skip_group_check=True)
                    pe.matmul(ps[:, lt, :], ones_row[:, :], browp.l[:, :], start=False, stop=False,
                              skip_group_check=True)
                with pe.Fori(0, C) as c:
                    g = bb * C + c
                    for i in range(2):
                        pe.wait_ge(sp1[i], g + 2)
                        ring.wait_free(pe, g, i)
                        for k in range(KC):
                            j = mm3(pe, ps[:, R_BANK + i, :], p1[i][:, k, :], XT[:, k, :], k == 0, k == KC - 1)
                        j.then_inc(ring.full, 1)
                    for i in range(2):
                        pe.wait_ge(sp2[i], g + 2)
                        pe.wait_ge(hid_done, g * 2 + i + 1)
                        for lt in range(LT):
                            j = mm3(pe, ps[:, lt, :], gp[:, i, lt * P:(lt + 1) * P], p2[i][:, :], False, False)
                        j.then_inc(prod_done, 1)
                barrier(pe, done, b)

            def act_(act, b):
                bb = b * 2 + nth
                with act.Fori(0, C) as c:
                    g = bb * C + c
                    for i in range(2):
                        ring.wait_full(act, g, i)
                        act.wait_ge(prod_done, g * 2 + i + 1)
                        apart(act)
                        act.activation(g32[:, i, :], ps[:, R_BANK + i, :], func,
                                       bias=cols[:, bass.ds(c * 2 + (c_b1 + i), 1)]).then_inc(ring.freed(i), 1)
                barrier(act, done, b)

            def dve_(dve, b):
                bb = b * 2 + nth
                dve.wait_ge(b_ld, bb * 16 + 16)
                dve.tensor_copy(browp.h[:, :], brow[:, :])
                dve.drain()
                dve.tensor_tensor(browp.l[:, :], brow[:, :], as_f32(browp.h[:, :]), ALU.subtract).then_inc(b_done, 1)
                with dve.Fori(0, C) as c:
                    g = bb * C + c
                    for i in range(2):
                        dve.wait_ge(ld2[i], g * 16 + 16)
                        dve.wait_ge(prod_done, g * 2 + i + 1)
                        dve.tensor_copy(p2[i].h[:, :], raw2[:, i, :]).then_inc(w2_hi, 1)
                        dve.wait_ge(w2_hi, g * 2 + i + 1)
                        dve.tensor_tensor(p2[i].l[:, :], raw2[:, i, :], as_f32(p2[i].h[:, :]),
                                          ALU.subtract).then_inc(sp2[i], 1)
                    for i in range(2):
                        ring.wait_done(dve, g, i)
                        dve.tensor_copy(gp.h[:, i, :], g32[:, i, :]).then_inc(g_hi, 1)
                        dve.wait_ge(g_hi, g * 2 + i + 1)
                        dve.tensor_tensor(gp.l[:, i, :], g32[:, i, :], as_f32(gp.h[:, i, :]),
                                          ALU.subtract).then_inc(hid_done, 1)
                dve.wait_ge(prod_done, bb * (2 * C) + (2 * C + 2))
                for lt in range(LT):
                    dve.tensor_tensor(res[:, lt, :], ps[:, lt, :], X[:, lt, :], ALU.add)
                dve.drain().then_inc(sum_done, 1)
                barrier(dve, done, b)

            add(sp_, pool_, pe_, act_, dve_)
            own.close()

        turn_1 = Turn(X, XT)
        bar = new_barrier()

        def turn_stage(turner, s):
            def sp_(sp, b):
                barrier(sp, s, b)

            def pool_(pool, b):
                barrier(pool, s, b)

            def pe_(pe, b):
                turner.pe(pe, b)
                barrier(pe, s, b)

            def act_(act, b):
                turner.act(act, b)
                barrier(act, s, b)

            def dve_(dve, b):
                turner.dve(dve, b)
                barrier(dve, s, b)

            add(sp_, pool_, pe_, act_, dve_)

        turn_stage(turn_1, bar)
        narrow("l1", X, 16, 4, NK, 0.25, at["bq_1"], at["bk_1"], at["bv_1"], t["L1_xattn_Wq"], t["L1_xattn_Wk"],
               t["L1_xattn_Wv"], t["L1_xattn_Wo"], t["L1_xattn_bo"], True)
        norm("n1", X, 1e-5, at["lns_1"], at["lno_1"], first=(t["L1_xattn_gamma"], t["L1_xattn_beta"], 1e-6))
        wide("1")
        norm("n2", X, 1e-5, at["lns_2"], at["lno_2"])
        wide("2")
        norm("n3", X, 1e-5, at["lns_m"], at["lno_m"])
        mlp(0, ACT.Gelu, t["L2_xattn_w_fc1"], t["L2_xattn_w_fc2"], at["b1_2"], t["L2_xattn_b_fc2"], False)
        turn_3 = Turn(X, XT)
        turn_stage(turn_3, new_barrier())
        l3 = ExitStack()
        acc3 = sb(l3, "acc3", [P, LT, D])
        narrow("l3", acc3, 32, 1, NK + NQ, 1.0 / 32, at["qb_3"], at["kb_3"], at["vb_3"], t["L3_xattn_q_w"],
               t["L3_xattn_kv_w"], None, t["L3_xattn_out_w"], t["L3_xattn_out_b"], False)
        norm("n4", acc3, 1e-6, at["pn_3"], None, rms=True)
        l3.close()
        mlp(1, ACT.Gelu_apprx_tanh, t["L3_xattn_mlp_w1"], t["L3_xattn_mlp_w2"], at["b1_3"], t["L3_xattn_mlp_b2"], True)

        pre = ExitStack()
        vec = sb(pre, "vec", [P, n_vt, P])
        pre.close()
        vec_clear = sem("vec_clear")

        def before_sp(sp):
            sp.wait_ge(vec_clear, 1)
            for r0_, n_, c_, w_, src in vec_rows:
                sp.dma_start(vec[r0_ % P:r0_ % P + n_, r0_ // P, c_:c_ + w_], src,
                             allow_slow_non_contiguous=src.ap[-1][0] != 1).then_inc(s_vec, 16)
            sp.dma_start(alpha[:, :], t["L0_xattn_alpha"].unsqueeze(0).broadcast_to([P, 1])).then_inc(s_vec, 16)

        def before_pool(pool):
            pool.memset(vec[:, :, :], 0.0).then_inc(vec_clear, 1)
            pool.memset(ident[:, :], 0.0).then_inc(s_pool, 1)
            pool.wait_ge(s_pool, 1)
            pool.affine_select(out=ident[:, :], in_=ident[:, :], compare_op=ALU.not_equal, fill=1.0, base=0,
                               pattern=[[-1, P]], channel_multiplier=1).then_inc(s_const, 1)
            pool.memset(zero_col[:, :], 0.0).then_inc(s_const, 1)
            pool.memset(ones_32[:, :], 1.0).then_inc(s_const, 1)
            pool.memset(as_f32(ones_row[:, :]), 1.0).then_inc(s_const, 1)

        def before_pe(pe):
            for ring_ in {r.full.name: r for r in credits}.values():
                ring_.credit(pe)
            for s in {s.name: s for s in extra_credits}.values():
                pe.sem_inc(s, 1)
            for s, n in deep_credits.values():
                pe.sem_inc(s, n)
            pe.wait_ge(s_const, 4)
            pe.wait_ge(s_vec, 16 * (len(vec_rows) + 1))
            for i in range(n_vt):
                m = pe.transpose(ps[:, 0, i * P:(i + 1) * P], vec[:, i, :], ident[:, :])
            m.then_inc(s_vt, 1)

        def before_dve(dve):
            dve.wait_ge(s_vt, 1)
            dve.tensor_copy(ident_r[:, :], ident[:, :]).then_inc(s_cols, 1)
            dve.tensor_copy(cols[:, :], ps[:, 0, 0:n_vt * P]).then_inc(s_cols, 1)

        block = ctx.enter_context(nc.Block())

        def all_stages(eng, name):
            eng.wait_ge(s_cols, 2)
            with eng.Fori(0, B) as b:
                for st in stages:
                    st[name](eng, b)

        @block.sync
        def _(sp):
            before_sp(sp)
            all_stages(sp, "sp")

        @block.gpsimd
        def _(pool):
            before_pool(pool)
            all_stages(pool, "pool")

        @block.tensor
        def _(pe):
            before_pe(pe)
            all_stages(pe, "pe")

        @block.scalar
        def _(act):
            all_stages(act, "act")

        @block.vector
        def _(dve):
            before_dve(dve)
            all_stages(dve, "dve")


def kernel(**inputs):
    import concourse.bacc as bacc
    from concourse.bass_utils import run_bass_kernel_spmd

    nc = bacc.Bacc("TRN2", target_bir_lowering=False, num_devices=1)
    arrays, t = {}, {}
    for name, value in inputs.items():
        a = np.ascontiguousarray(value).reshape(np.shape(value) or (1,))
        arrays["in_" + name] = a
        t[name] = nc.dram_tensor("in_" + name, a.shape, mybir.dt.from_np(a.dtype), kind="ExternalInput").ap()
    out = nc.dram_tensor("out_0", (B, NQ, D), F32, kind="ExternalOutput").ap()
    build(nc, t, out)
    r = run_bass_kernel_spmd(nc, [arrays], core_ids=[0])
    return r.results[0]["out_0"]
```
